# Optimizing a Trainium2 kernel written in Bass

```python
import numpy as np
import jax
import jax.numpy as jnp

def _softmax(x, axis=-1):
    return jax.nn.softmax(x, axis=axis)

def _gelu(x):
    return jax.nn.gelu(x, approximate=True)

def _silu(x):
    return jax.nn.silu(x)

def _sigmoid(x):
    return jax.nn.sigmoid(x)

def _layernorm(x, axis=-1, eps=1e-05):
    m = jnp.mean(x, axis=axis, keepdims=True)
    v = jnp.var(x, axis=axis, keepdims=True)
    return (x - m) / jnp.sqrt(v + eps)

def _scatter_add(tgt, idx, src, axis=0):
    return tgt.at[idx].add(src)

def _segment_sum(src, seg, n):
    return jax.ops.segment_sum(src, seg, n)
kernel_name = 'mk_decoder_postln_d2_seqx_r8_800237'

def setup_inputs(seed: int=0):
    np.random.seed(seed)
    _w = jnp.asarray

    def _rec_inputs():
        import jax
        import jax.numpy as jnp
        _rk = jax.random.key(seed)
        x = 7.22e-05 + 1 * jax.random.normal(jax.random.fold_in(_rk, 1), (4, 512, 128), jnp.float32)
        _lenS = 512 - jax.random.randint(jax.random.fold_in(_rk, 7), (4,), 0, max(1, 512 // 4) + 1, jnp.int32)
        _lenS2 = 77 - jax.random.randint(jax.random.fold_in(_rk, 8), (4,), 0, max(1, 77 // 4) + 1, jnp.int32)
        _ctx_1024P = jax.random.normal(jax.random.fold_in(_rk, 11), (4, 16, 128), jnp.float32)
        _ctx_1024c = jax.random.dirichlet(jax.random.fold_in(_rk, 511), 0.3 * jnp.ones((16,), jnp.float32), (4, 77))
        _ctx_1024t = jnp.einsum('bsk,bkd->bsd', _ctx_1024c, _ctx_1024P)
        _ctx_1024t = _ctx_1024t * jax.lax.rsqrt(jnp.mean(jnp.square(_ctx_1024t)) + 1e-12) * 0.953939
        ctx_1024 = 4.13588e-05 + 0.999923 * (_ctx_1024t + 0.3 * jax.random.normal(jax.random.fold_in(_rk, 611), (4, 77, 128), jnp.float32))
        return (x, ctx_1024)
    x, ctx_1024 = _rec_inputs()

    def _L0_attn_setup():
        import jax, jax.numpy as jnp
        import numpy as np
        B, S, E = (4, 256, 128)
        HIDDEN = 128
        HEADS = 16
        key = jax.random.key(seed)
        k0, k1, k2, k3, k4 = jax.random.split(key, 5)
        inputs = jax.random.normal(k0, (B, S, E), dtype=jnp.float32)
        W_qkv = jax.random.normal(k1, (E, 3 * HIDDEN), dtype=jnp.float32) * 0.02
        b_qkv = jnp.zeros((3 * HIDDEN,), dtype=jnp.float32)
        W_out = jax.random.normal(k2, (HIDDEN, HIDDEN), dtype=jnp.float32) * 0.02
        b_out = jnp.zeros((HIDDEN,), dtype=jnp.float32)
        return {'inputs': inputs, 'W_qkv': W_qkv, 'b_qkv': b_qkv, 'W_out': W_out, 'b_out': b_out}
    _L0_attn_all = _L0_attn_setup()
    _L0_attn_in = {k: v for k, v in _L0_attn_all.items() if k in ('W_qkv', 'b_qkv', 'W_out', 'b_out')}
    del _L0_attn_all

    def _L0_xattn_setup():
        import jax, jax.numpy as jnp
        import numpy as np
        D_MODEL = 128
        NUM_HEADS = 16

        def _split(x, h):
            B, S, D = x.shape
            return x.reshape(B, S, h, D // h).transpose(0, 2, 1, 3)
        key = jax.random.key(seed)
        ks = jax.random.split(key, 12)
        B, S, D = (4, 256, D_MODEL)
        s = 1.0 / np.sqrt(D)
        inp = {'q': jax.random.normal(ks[0], (B, S, D), jnp.float32), 'k': jax.random.normal(ks[1], (B, S, D), jnp.float32), 'v': jax.random.normal(ks[2], (B, S, D), jnp.float32), 'wq': jax.random.normal(ks[3], (D, D), jnp.float32) * s, 'bq': jnp.zeros((D,), jnp.float32), 'wk': jax.random.normal(ks[4], (D, D), jnp.float32) * s, 'bk': jnp.zeros((D,), jnp.float32), 'wv': jax.random.normal(ks[5], (D, D), jnp.float32) * s, 'bv': jnp.zeros((D,), jnp.float32), 'wo': jax.random.normal(ks[6], (D, D), jnp.float32) * s, 'bo': jnp.zeros((D,), jnp.float32)}
        return inp
    _L0_xattn_all = _L0_xattn_setup()
    _L0_xattn_in = {k: v for k, v in _L0_xattn_all.items() if k in ('wq', 'bq', 'wk', 'bk', 'wv', 'bv', 'wo', 'bo')}
    del _L0_xattn_all

    def _L0_ffn_setup():
        import jax, jax.numpy as jnp
        import numpy as np
        B, S, D, E, F = (2, 128, 128, 14, 256)
        key = jax.random.key(seed)
        k0, k1, k2, k3 = jax.random.split(key, 4)
        h = jax.random.normal(k0, (B, S, D), jnp.float32)
        gate_w = jax.random.normal(k1, (E, D), jnp.float32) * 0.02
        w1 = jax.random.normal(k2, (E, D, F), jnp.float32) * (1.0 / np.sqrt(D).astype(np.float32))
        b1 = jnp.zeros((E, F), jnp.float32)
        w2 = jax.random.normal(k3, (E, F, D), jnp.float32) * (1.0 / np.sqrt(F).astype(np.float32))
        b2 = jnp.zeros((E, D), jnp.float32)
        return {'h': h, 'gate_w': gate_w, 'w1': w1, 'b1': b1, 'w2': w2, 'b2': b2}
    _L0_ffn_all = _L0_ffn_setup()
    _L0_ffn_in = {k: v for k, v in _L0_ffn_all.items() if k in ('gate_w', 'w1', 'b1', 'w2', 'b2')}
    del _L0_ffn_all

    def _L1_attn_setup():
        import jax, jax.numpy as jnp
        import numpy as np
        DIM = 128
        H = 16
        HD = DIM // H
        EPS_DENOM = 1e-06
        EPS_LN = 1e-05
        key = jax.random.key(seed)
        ks = jax.random.split(key, 8)
        B, N = (4, 512)
        s = 1.0 / np.sqrt(DIM)
        return {'x': jax.random.normal(ks[0], (B, N, DIM), dtype=jnp.float32), 'Wq': jax.random.normal(ks[1], (DIM, DIM), dtype=jnp.float32) * s, 'bq': jnp.zeros((DIM,), dtype=jnp.float32), 'Wk': jax.random.normal(ks[2], (DIM, DIM), dtype=jnp.float32) * s, 'bk': jnp.zeros((DIM,), dtype=jnp.float32), 'Wv': jax.random.normal(ks[3], (DIM, DIM), dtype=jnp.float32) * s, 'bv': jnp.zeros((DIM,), dtype=jnp.float32), 'gamma': jnp.ones((DIM,), dtype=jnp.float32), 'beta': jnp.zeros((DIM,), dtype=jnp.float32)}
    _L1_attn_all = _L1_attn_setup()
    _L1_attn_in = {k: v for k, v in _L1_attn_all.items() if k in ('Wq', 'bq', 'Wk', 'bk', 'Wv', 'bv', 'gamma', 'beta')}
    del _L1_attn_all

    def _L1_xattn_setup():
        import jax, jax.numpy as jnp
        import numpy as np
        HEADS = 8
        DIM_HEAD = 64
        SCALE = 8.0
        EPS = 1e-05

        def layer_norm(x, g, b):
            mu = jnp.mean(x, axis=-1, keepdims=True)
            var = jnp.mean((x - mu) ** 2, axis=-1, keepdims=True)
            return (x - mu) * jax.lax.rsqrt(var + EPS) * g + b
        key = jax.random.key(seed)
        ks = jax.random.split(key, 6)
        b, n, dim = (4, 512, 128)
        inner = HEADS * DIM_HEAD
        return {'x': jax.random.normal(ks[0], (b, n, dim), jnp.float32), 'context': jax.random.normal(ks[1], (b, n, dim), jnp.float32), 'Wq': jax.random.normal(ks[2], (dim, inner), jnp.float32) * 0.03, 'Wkv': jax.random.normal(ks[3], (dim, 2 * inner), jnp.float32) * 0.03, 'null_kv': jax.random.normal(ks[4], (2, DIM_HEAD), jnp.float32), 'ln_q_g': jnp.ones((inner,), jnp.float32), 'ln_q_b': jnp.zeros((inner,), jnp.float32), 'ln_out_g': jnp.ones((inner,), jnp.float32), 'ln_out_b': jnp.zeros((inner,), jnp.float32), 'Wout': jax.random.normal(ks[5], (inner, dim), jnp.float32) * 0.03}
    _L1_xattn_all = _L1_xattn_setup()
    _L1_xattn_in = {k: v for k, v in _L1_xattn_all.items() if k in ('Wq', 'Wkv', 'null_kv', 'ln_q_g', 'ln_q_b', 'ln_out_g', 'ln_out_b', 'Wout')}
    del _L1_xattn_all

    def _L1_ffn_setup():
        import jax, jax.numpy as jnp
        import numpy as np
        DIM = 128

        def _reference_tuple_inner(x, W_r, W_k, W_v, mu_r, mu_k):
            B, T, C = x.shape
            x_prev = jnp.concatenate([jnp.zeros((B, 1, C), x.dtype), x[:, :-1, :]], axis=1)
            xr = mu_r * x + (1.0 - mu_r) * x_prev
            xk = mu_k * x + (1.0 - mu_k) * x_prev
            r = jax.nn.sigmoid(jnp.einsum('btc,dc->btd', xr, W_r))
            k = jnp.einsum('btc,dc->btd', xk, W_k)
            k_act = jnp.square(jax.nn.relu(k))
            out = r * jnp.einsum('btc,dc->btd', k_act, W_v)
            new_state = x[:, -1, :]
            return (out, new_state)
        key = jax.random.key(seed)
        ks = jax.random.split(key, 6)
        B, T, C = (8, 256, DIM)
        x = jax.random.normal(ks[0], (B, T, C), dtype=jnp.float32)
        s = 1.0 / np.sqrt(C)
        W_r = jax.random.uniform(ks[1], (C, C), jnp.float32, -s, s)
        W_k = jax.random.uniform(ks[2], (C, C), jnp.float32, -s, s)
        W_v = jax.random.uniform(ks[3], (C, C), jnp.float32, -s, s)
        mu_r = jax.random.uniform(ks[4], (C,), jnp.float32)
        mu_k = jax.random.uniform(ks[5], (C,), jnp.float32)
        return {'x': x, 'W_r': W_r, 'W_k': W_k, 'W_v': W_v, 'mu_r': mu_r, 'mu_k': mu_k}
    _L1_ffn_all = _L1_ffn_setup()
    _L1_ffn_in = {k: v for k, v in _L1_ffn_all.items() if k in ('W_r', 'W_k', 'W_v', 'mu_r', 'mu_k')}
    del _L1_ffn_all
    return {'x': x, 'ctx_1024': ctx_1024, 'L0_attn_W_qkv': _L0_attn_in['W_qkv'], 'L0_attn_b_qkv': _L0_attn_in['b_qkv'], 'L0_attn_W_out': _L0_attn_in['W_out'], 'L0_attn_b_out': _L0_attn_in['b_out'], 'L0_xattn_wq': _L0_xattn_in['wq'], 'L0_xattn_bq': _L0_xattn_in['bq'], 'L0_xattn_wk': _L0_xattn_in['wk'], 'L0_xattn_bk': _L0_xattn_in['bk'], 'L0_xattn_wv': _L0_xattn_in['wv'], 'L0_xattn_bv': _L0_xattn_in['bv'], 'L0_xattn_wo': _L0_xattn_in['wo'], 'L0_xattn_bo': _L0_xattn_in['bo'], 'L0_ffn_gate_w': _L0_ffn_in['gate_w'], 'L0_ffn_w1': _L0_ffn_in['w1'], 'L0_ffn_b1': _L0_ffn_in['b1'], 'L0_ffn_w2': _L0_ffn_in['w2'], 'L0_ffn_b2': _L0_ffn_in['b2'], 'L1_attn_Wq': _L1_attn_in['Wq'], 'L1_attn_bq': _L1_attn_in['bq'], 'L1_attn_Wk': _L1_attn_in['Wk'], 'L1_attn_bk': _L1_attn_in['bk'], 'L1_attn_Wv': _L1_attn_in['Wv'], 'L1_attn_bv': _L1_attn_in['bv'], 'L1_attn_gamma': _L1_attn_in['gamma'], 'L1_attn_beta': _L1_attn_in['beta'], 'L1_xattn_Wq': _L1_xattn_in['Wq'], 'L1_xattn_Wkv': _L1_xattn_in['Wkv'], 'L1_xattn_null_kv': _L1_xattn_in['null_kv'], 'L1_xattn_ln_q_g': _L1_xattn_in['ln_q_g'], 'L1_xattn_ln_q_b': _L1_xattn_in['ln_q_b'], 'L1_xattn_ln_out_g': _L1_xattn_in['ln_out_g'], 'L1_xattn_ln_out_b': _L1_xattn_in['ln_out_b'], 'L1_xattn_Wout': _L1_xattn_in['Wout'], 'L1_ffn_W_r': _L1_ffn_in['W_r'], 'L1_ffn_W_k': _L1_ffn_in['W_k'], 'L1_ffn_W_v': _L1_ffn_in['W_v'], 'L1_ffn_mu_r': _L1_ffn_in['mu_r'], 'L1_ffn_mu_k': _L1_ffn_in['mu_k']}

def reference(x, ctx_1024, L0_attn_W_qkv, L0_attn_b_qkv, L0_attn_W_out, L0_attn_b_out, L0_xattn_wq, L0_xattn_bq, L0_xattn_wk, L0_xattn_bk, L0_xattn_wv, L0_xattn_bv, L0_xattn_wo, L0_xattn_bo, L0_ffn_gate_w, L0_ffn_w1, L0_ffn_b1, L0_ffn_w2, L0_ffn_b2, L1_attn_Wq, L1_attn_bq, L1_attn_Wk, L1_attn_bk, L1_attn_Wv, L1_attn_bv, L1_attn_gamma, L1_attn_beta, L1_xattn_Wq, L1_xattn_Wkv, L1_xattn_null_kv, L1_xattn_ln_q_g, L1_xattn_ln_q_b, L1_xattn_ln_out_g, L1_xattn_ln_out_b, L1_xattn_Wout, L1_ffn_W_r, L1_ffn_W_k, L1_ffn_W_v, L1_ffn_mu_r, L1_ffn_mu_k):
    import jax
    import jax.numpy as jnp

    def _L0_attn_ref(inputs, W_qkv, b_qkv, W_out, b_out):
        import jax, jax.numpy as jnp
        import numpy as np
        B, S, E = (4, 256, 128)
        HIDDEN = 128
        HEADS = 16
        Bv, Sv, Ev = inputs.shape
        x = inputs @ W_qkv + b_qkv
        x = x.reshape(Bv, HEADS, Sv, -1)
        q, k, v = jnp.split(x, 3, axis=-1)
        scale = (2 * HIDDEN) ** (-0.5)
        qk = jnp.einsum('bhse,bhte->bhst', q, k) * scale
        mask = jnp.triu(jnp.full((Sv, Sv), -jnp.inf, dtype=qk.dtype), k=1)
        attn = jax.nn.softmax(qk + mask, axis=-1)
        sa = jnp.einsum('bhst,bhte->bhse', attn, v).reshape(Bv, Sv, -1)
        return sa @ W_out + b_out

    def _L0_xattn_ref(q, k, v, wq, bq, wk, bk, wv, bv, wo, bo):
        import jax, jax.numpy as jnp
        import numpy as np
        D_MODEL = 128
        NUM_HEADS = 16

        def _split(x, h):
            B, S, D = x.shape
            return x.reshape(B, S, h, D // h).transpose(0, 2, 1, 3)
        h = NUM_HEADS
        qp = _split(q @ wq.T + bq, h)
        kp = _split(k @ wk.T + bk, h)
        vp = _split(v @ wv.T + bv, h)
        dh = qp.shape[-1]
        scale = 1.0 / jnp.sqrt(jnp.asarray(dh, qp.dtype))
        score = jnp.einsum('bhqd,bhkd->bhqk', qp, kp) * scale
        attn = jax.nn.softmax(score, axis=-1)
        val = jnp.einsum('bhqk,bhkd->bhqd', attn, vp)
        B, _, S, _ = val.shape
        out = val.transpose(0, 2, 1, 3).reshape(B, S, h * dh)
        return out @ wo.T + bo

    def _L0_ffn_ref(h, gate_w, w1, b1, w2, b2):
        import jax, jax.numpy as jnp
        import numpy as np
        B, S, D, E, F = (2, 128, 128, 14, 256)
        Bb, Ss, Dd = h.shape
        x = h.reshape(Bb * Ss, Dd)
        logits = x @ gate_w.T
        probs = jax.nn.softmax(logits, axis=-1)
        top2_p, top2_i = jax.lax.top_k(probs, 2)
        w = top2_p / jnp.maximum(top2_p.sum(-1, keepdims=True), 1e-10)
        hh = jnp.einsum('nd,edf->nef', x, w1) + b1
        hh = jax.nn.gelu(hh, approximate=False)
        all_out = jnp.einsum('nef,efd->ned', hh, w2) + b2
        n = jnp.arange(x.shape[0])
        out0 = all_out[n, top2_i[:, 0]]
        out1 = all_out[n, top2_i[:, 1]]
        moe_out = w[:, 0:1] * out0 + w[:, 1:2] * out1
        result = jnp.clip(x + moe_out, -100.0, 100.0).reshape(Bb, Ss, Dd)
        return result

    def _L1_attn_ref(x, Wq, bq, Wk, bk, Wv, bv, gamma, beta):
        import jax, jax.numpy as jnp
        import numpy as np
        DIM = 128
        H = 16
        HD = DIM // H
        EPS_DENOM = 1e-06
        EPS_LN = 1e-05
        B, N, C = x.shape
        q = (x @ Wq.T + bq).reshape(B, N, H, HD)
        k = (x @ Wk.T + bk).reshape(B, N, H, HD)
        v = (x @ Wv.T + bv).reshape(B, N, H, HD)
        q = jax.nn.relu(q)
        k = jax.nn.relu(k)
        kv = jnp.einsum('bnhd,bnhp->bhdp', k, v)
        k_sum = k.sum(axis=1)
        denom = jnp.einsum('bnhd,bhd->bnh', q, k_sum)
        denom = jnp.maximum(denom, EPS_DENOM)[..., None]
        ctx = jnp.einsum('bnhd,bhdp->bnhp', q, kv)
        out = (ctx / denom).reshape(B, N, C)
        y = out + x
        mu = y.mean(axis=-1, keepdims=True)
        var = y.var(axis=-1, keepdims=True)
        return (y - mu) / jnp.sqrt(var + EPS_LN) * gamma + beta

    def _L1_xattn_ref(x, context, Wq, Wkv, null_kv, ln_q_g, ln_q_b, ln_out_g, ln_out_b, Wout):
        import jax, jax.numpy as jnp
        import numpy as np
        HEADS = 8
        DIM_HEAD = 64
        SCALE = 8.0
        EPS = 1e-05

        def layer_norm(x, g, b):
            mu = jnp.mean(x, axis=-1, keepdims=True)
            var = jnp.mean((x - mu) ** 2, axis=-1, keepdims=True)
            return (x - mu) * jax.lax.rsqrt(var + EPS) * g + b
        b, n, _ = x.shape
        m = context.shape[1]
        h, d = (HEADS, DIM_HEAD)
        q = x @ Wq
        kv = context @ Wkv
        k, v = jnp.split(kv, 2, axis=-1)
        q = layer_norm(q, ln_q_g, ln_q_b)
        split = lambda t: t.reshape(t.shape[0], t.shape[1], h, d).transpose(0, 2, 1, 3)
        q, k, v = (split(q), split(k), split(v))
        nk = jnp.broadcast_to(null_kv[0], (b, h, 1, d))
        nv = jnp.broadcast_to(null_kv[1], (b, h, 1, d))
        k = jnp.concatenate([nk, k], axis=2)
        v = jnp.concatenate([nv, v], axis=2)
        q = jax.nn.softmax(q, axis=-1) * SCALE
        k = jax.nn.softmax(k, axis=2)
        ctx = jnp.einsum('bhnd,bhne->bhde', k, v)
        out = jnp.einsum('bhnd,bhde->bhne', q, ctx)
        out = out.transpose(0, 2, 1, 3).reshape(b, n, h * d)
        out = layer_norm(out, ln_out_g, ln_out_b)
        return out @ Wout

    def _L1_ffn_ref(x, W_r, W_k, W_v, mu_r, mu_k):
        import jax, jax.numpy as jnp
        import numpy as np
        DIM = 128

        def _reference_tuple_inner(x, W_r, W_k, W_v, mu_r, mu_k):
            B, T, C = x.shape
            x_prev = jnp.concatenate([jnp.zeros((B, 1, C), x.dtype), x[:, :-1, :]], axis=1)
            xr = mu_r * x + (1.0 - mu_r) * x_prev
            xk = mu_k * x + (1.0 - mu_k) * x_prev
            r = jax.nn.sigmoid(jnp.einsum('btc,dc->btd', xr, W_r))
            k = jnp.einsum('btc,dc->btd', xk, W_k)
            k_act = jnp.square(jax.nn.relu(k))
            out = r * jnp.einsum('btc,dc->btd', k_act, W_v)
            new_state = x[:, -1, :]
            return (out, new_state)
        return _reference_tuple_inner(x, W_r, W_k, W_v, mu_r, mu_k)[0]
    x = _layernorm(x + _L0_attn_ref(x, L0_attn_W_qkv, L0_attn_b_qkv, L0_attn_W_out, L0_attn_b_out), axis=-1)
    x = _layernorm(x + _L0_xattn_ref(x, ctx_1024, ctx_1024, L0_xattn_wq, L0_xattn_bq, L0_xattn_wk, L0_xattn_bk, L0_xattn_wv, L0_xattn_bv, L0_xattn_wo, L0_xattn_bo), axis=-1)
    x = _layernorm(x + _L0_ffn_ref(x, L0_ffn_gate_w, L0_ffn_w1, L0_ffn_b1, L0_ffn_w2, L0_ffn_b2), axis=-1)
    x = _layernorm(x + _L1_attn_ref(x, L1_attn_Wq, L1_attn_bq, L1_attn_Wk, L1_attn_bk, L1_attn_Wv, L1_attn_bv, L1_attn_gamma, L1_attn_beta), axis=-1)
    x = _layernorm(x + _L1_xattn_ref(x, ctx_1024, L1_xattn_Wq, L1_xattn_Wkv, L1_xattn_null_kv, L1_xattn_ln_q_g, L1_xattn_ln_q_b, L1_xattn_ln_out_g, L1_xattn_ln_out_b, L1_xattn_Wout), axis=-1)
    x = _layernorm(x + _L1_ffn_ref(x, L1_ffn_W_r, L1_ffn_W_k, L1_ffn_W_v, L1_ffn_mu_r, L1_ffn_mu_k), axis=-1)
    return x

_drawn_inputs = setup_inputs


def setup_inputs(seed=0):
    import zlib

    import numpy as np

    out = dict(_drawn_inputs(seed))
    spreads = {'L0_attn_b_qkv': (0.0, 0.773),
     'L0_attn_b_out': (0.0, 0.1),
     'L0_xattn_bq': (0.0, 0.1),
     'L0_xattn_bk': (0.0, 2.0),
     'L0_xattn_bv': (0.0, 0.1),
     'L0_xattn_bo': (0.0, 0.1),
     'L0_ffn_b1': (0.0, 0.42),
     'L0_ffn_b2': (0.0, 0.278),
     'L1_attn_bq': (0.0, 2.0),
     'L1_attn_bk': (0.0, 2.0),
     'L1_attn_bv': (0.0, 0.1),
     'L1_attn_gamma': (1.0, 0.2),
     'L1_attn_beta': (0.0, 0.1),
     'L1_xattn_ln_q_g': (1.0, 0.6),
     'L1_xattn_ln_q_b': (0.0, 2.0),
     'L1_xattn_ln_out_g': (1.0, 0.2),
     'L1_xattn_ln_out_b': (0.0, 0.1)}
    factors = {'L0_attn_W_qkv': 4.952, 'L0_attn_W_out': 4.149, 'L1_xattn_Wq': 3.241, 'L1_ffn_mu_r': 7.285}
    for name, (base, spread) in spreads.items():
        noise = np.random.default_rng([zlib.crc32(name.encode()), seed]).standard_normal(out[name].shape)
        drawn = base * np.exp(spread * noise) if base else spread * noise
        out[name] = jnp.asarray(drawn.astype(out[name].dtype))
    for name, factor in factors.items():
        out[name] = (out[name] * factor).astype(out[name].dtype)
    return out
```

```python
from contextlib import ExitStack

import numpy as np
import concourse.bass as bass
from concourse import mybir
from concourse.alu_op_type import AluOpType as ALU

ACT=mybir.ActivationFunctionType; AX=mybir.AxisListType
F32=mybir.dt.float32; BF16=mybir.dt.bfloat16
P=128; NT=16; H4=4; C=16; DH=8; NP=512
BIG=-1e30
NB=4; L=77; LG=4*L; NE=14; F=256; EP=16; NQ=512
class Sem:
    def __init__(self, sem, per): self.sem, self.per = sem, per
    def upto(self, t, n=0):
        return t * self.per + n

class Step:
    def __init__(self, i, k): self.i, self.k = i, k
    def __sub__(self, d): return Step(self.i, self.k - d)
    def __add__(self, d): return Step(self.i, self.k + d)
    @property
    def n(self): return self.k if self.i is None else self.i * 4 + self.k
    @property
    def half(self): return self.k // 2 if self.i is None else self.i * 2 + self.k // 2
    @property
    def p(self): return self.k % 2
    @property
    def q(self): return self.k % 4
    def first(self, n): return self.i is None and self.k < n

def wait(e, s, t, n=0):
    v = s.upto(t.n, n)
    if isinstance(v, int) and v <= 0:
        return
    e.wait_ge(s.sem, v)

def wait_apart(e, s, t, n=0):
    wait(e, s, t, n)
    if t.i is not None:
        e.nop(nofuse=True)

def wait_dma(e, s, t):
    if t.first(0): return
    s = s[t.p]
    e.wait_ge(s.sem, (t.half + 1) * s.per)

def wait_dma_apart(e, s, t):
    wait_dma(e, s, t)
    if t.i is not None:
        e.nop(nofuse=True)

UNITS_S = [(0,[0,1,2,3]),(1,[0,1]),(1,[2,3])]+[(2,[r]) for r in range(4)]+[(3,[r]) for r in range(4)]
UNITS_T = [(0,[r]) for r in range(4)]+[(1,[r]) for r in range(4)]+[(2,[0,1]),(2,[2,3]),(3,[0,1,2,3])]

CW=[128,128,52]
PER=dict(ctx_in=16, vb_in=96, x1b=1, kT_sb=1, v_sb=1, kf=1, khi=1, qf=1, qhi=1, mxd=12, m_sb=1, exp2=12, rD=1, On=1, xp=6, mv=6, vep=6, rs=6,
  x2=4, x2T=1, lg=1, e0=1, esub=1, ge=1, G=1, GT=1, gelu=28, accd=15, x3=4, x3T=1, kvs=2, kr=1, kvm=2, q1=1, g4=4, x4=4, x4T=1,
  k5=1, k5n=4, k5m=1, k5e=4, k5s=1, kn=1, v5=1, cx=2, mvq=4, z5=4, zg=4, zsub=4, e5=4, eT=4, o5=4, z2=4, zT=4, x5=4, x5T=1, xk=1, xr=1, kr6=1, kact=1, sg=1, x6=4,
  vq=4, rq=4, nq=4, mvo=4, vo=4, ro=4, no=4,
  p_kT=1,p_v=1,p_qT=1,p_S=12,p_m=1,p_T=12,p_pv=3,p_y2=1,p_x2T=1,p_lg=1,p_H=28,p_E=14,p_GT=1,p_b2=1,p_x3T=1,p_kv=2,p_q1=1,p_kvm=1,p_ctx=2,p_x4T=1,
  p_k5=1,p_v5=1,p_kn=1,p_cx=1,p_q5=4,p_eT=4,p_o5=4,p_zT=4,p_w5=4,p_x5T=1,p_k6=1,p_r6=1,p_v6=1, out=16, dv=141, xm=2)


def build(nc, CN, RN, out, D):
    scr_t2 = nc.dram_tensor("scr_t2",(2,P,2*NP),BF16).ap()
    scr_v = nc.dram_tensor("scr_v",(2,P,P),F32).ap()
    with ExitStack() as ctx:
        sb=lambda n,s,t=F32: ctx.enter_context(nc.sbuf_tensor(n,s,t))
        def sem(n,per): return Sem(ctx.enter_context(nc.semaphore(n)),per)
        def sem2(n,per): return [sem(n+'0',per),sem(n+'1',per)]
        bank=[ctx.enter_context(nc.psum_tensor(f"bank{k}",[P,512],F32)) for k in range(8)]
        ps_proj=bank[0]; ps_mT=bank[0]; ps_post=bank[1]; ps_S=bank[2:4]; ps_T=bank[4:6]; ps_O=bank[6:8]
        idf=sb("idf",[P,P])
        idb=sb("idb",[P,P],BF16)
        x1=sb("x1",[P,NT,P])
        x1T=sb("x1T",[P,NT*P])
        Pr=sb("Pr",[P,2,H4,NP])
        mhalf=sb("mhalf",[P,4])
        vep_d=sem("vep_d",1)
        w_in=sem("w_in",0); consts=sem("consts",0); zeros=sem("zeros",0); xb_done=sem("xb_done",0)
        xt_in=sem2("xt_in",16); proj=sem("proj",1); qkv_done=sem("qkv_done",1); part1=sem("part1",1)
        dprep=sem("dprep",4)
        t2_done=sem("t2_done",1); t2_out=sem2("t2_out",16); v_out=sem2("v_out",16); qk_in=sem2("qk_in",96); v_in=sem2("v_in",16)
        s_ready=sem("s_ready",11); s_max=sem("s_max",11); m_tr=sem("m_tr",1); m_cp=sem("m_cp",1); m_in=sem2("m_in",16)
        st_ready=sem("st_ready",11); p_exp=sem("p_exp",11); p_sel=sem("p_sel",4); pv=sem("pv",4)
        o_tr=sem("o_tr",1); o_rc=sem("o_rc",1); ao_done=sem("ao_done",1); aoT_ps=sem("aoT_ps",1); aoT_sb=sem("aoT_sb",1); y_ps=sem("y_ps",1)
        x1p_d=sem("x1p_d",1); st_d=sem("st_d",1); mv_d=sem("mv_d",1); rstd_d=sem("rstd_d",1); x1_d=sem("x1_d",1); x1T_ps=sem("x1T_ps",1); x1T_sb=sem("x1T_sb",1); x1_cp=sem("x1_cp",1)
        outs=sem("outs",0)
        sems={}
        for k,v in PER.items(): sems[k]=ctx.enter_context(nc.semaphore("s_"+k))
        bk=bank
        def W(e,b,name,n):
            per=PER[name]; n=max(n,0)
            if b.i is None:
                v=b.k*per+n
                if v<=0: return
                e.wait_ge(sems[name],v)
            else: e.wait_ge(sems[name], b.n1*per+n)
        def WA(e,b,name,n):
            W(e,b,name,n)
            if b.i is not None: e.nop(nofuse=True)
        wB_in=ctx.enter_context(nc.semaphore("wB_in")); constsB=ctx.enter_context(nc.semaphore("constsB")); zerosB=ctx.enter_context(nc.semaphore("zerosB")); pre=ctx.enter_context(nc.semaphore("pre")); fin=ctx.enter_context(nc.semaphore("fin"))
        sel=sb("sel",[P,4,LG],BF16); selp=sb("selp",[P,4,4,L]); 
        obl=sb("obl",[P,3,4,DH]); blk8=sb("blk8",[P,16,DH])
        names_w=dict(wq=P,wk=P,wv=P,wo=P,gate=NE,w1=NE*F,w2=NE*2*P,wkv1=256,wq1=P,Wq5=512,Wk5=512,Wv5=512,Wo5=512,Wr=P,Wk6=P,Wv6=P,cols=D['cols'].shape[1])
        wt={n:sb("w_"+n,[P,k]) for n,k in names_w.items()}
        col=lambda n,j=0: wt['cols'][:,CN[n]+j:CN[n]+j+1]
        nrow=D['rows'].shape[1]
        rows=sb("rows",[P,nrow])
        row=lambda n,k: rows[:,RN[n]:RN[n]+k]
        b2=sb("b2",[NE,P]); 
        wo5=sb("wo5",[P,4,P]); wb5=sb("wb5",[P,P]); onemu=sb("onemu",[P,2])
        with ExitStack() as first:
            sa=lambda n,s,t=F32: first.enter_context(nc.sbuf_tensor(n,s,t))
            maskT=sa("maskT",[P,P],BF16)
            maskf=sa("maskf",[P,P])
            wqkv_s=sa("wqkv_s",[P,384])
            wout_s=sa("wout_s",[P,P])
            bqkv_s=sa("bqkv_s",[P,384])
            bout_s=sa("bout_s",[P,P])
            xb=sa("xb",[P,NT,P])
            xT_s=sa("xT_s",[P,2,P])
            qkv=sa("qkv",[P,2,384])
            part=sa("part",[P,2,2,C,32],BF16)
            res1=sa("res1",[P,2,256])
            t2=sa("t2",[P,2,2,NP],BF16)
            QX=sa("QX",[P,4,H4,NP],BF16)
            KX=sa("KX",[P,4,H4,NP],BF16)
            Vx=sa("Vx",[P,4,16,32])
            mx=sa("mx",[P,2,16],BF16)
            mT=sa("mT",[16,P],BF16)
            OT=sa("OT",[P,C,32])
            rc=sa("rc",[P,C])
            ao=sa("ao",[P,C,DH])
            aoT=sa("aoT",[P,P])
            x1p=sa("x1p",[P,P])
            st=sa("st",[P,6])
            mv=sa("mv",[P,2])
            rstd=sa("rstd",[P,1])
            vep=sa("vep",[P,1])
            x1s=sa("x1s",[P,P])
        ctx_s=sb("ctx_s",[P,L]); kT_s=sb("kT_s",[P,L]); v_s=sb("v_s",[L,P])
        Kf=sb("Kf",[P,4,LG]); Khi=sb("Khi",[P,16*L],BF16); Vb=sb("Vb",[P,4,3,32])
        qf=sb("qf",[P,NQ]); qhi=sb("qhi",[P,NQ],BF16); mx2=sb("mx2",[P,4,P],BF16); mT2=sb("mT2",[P,NQ],BF16)
        rD=sb("rD",[P,NQ]); On=sb("On",[P,NQ])
        x1b=sb("x1b",[P,4,P]); xp=sb("xp",[P,4,P]); stb=sb("stb",[P,4,6]); mvb=sb("mvb",[P,4,2]); vepb=sb("vepb",[P,4]); rstdb=sb("rstdb",[P,4])
        x2=sb("x2",[P,4,P]); x2T=sb("x2T",[P,NQ]); lg=sb("lg",[P,4,NE]); t8=sb("t8",[P,4,8]); p8=sb("p8",[P,4,8]); lr=sb("lr",[P,4,NE]); msk=sb("msk",[P,4,NE]); es=sb("es",[P,4,NE]); ge=sb("ge",[P,4,NE]); G=sb("G",[P,4,NE]); gz=sb("gz",[P,4]); gr=sb("gr",[P,4])
        GT=sb("GT",[NE,NQ]); Hb=sb("Hb",[P,2,2,NQ]); acc=sb("acc",[P,4,P])
        x3=sb("x3",[P,4,P]); x3T=sb("x3T",[P,NQ]); kvs=sb("kvs",[P,4,257]); kvm=sb("kvm",[P,144]); q1s=sb("q1s",[P,NQ]); dn=sb("dn",[P,4,16]); y4=sb("y4",[P,4,P])
        x4=sb("x4",[P,4,P]); x4T=sb("x4T",[P,NQ])
        k5=sb("k5",[P,4,L+1]); k5m=sb("k5m",[P,4]); k5e=sb("k5e",[P,4,L+1]); k5s=sb("k5s",[P,4]); kn=sb("kn",[L+1,512]); vn=sb("vn",[L+1,512]); cx=sb("cx",[P,4,P])
        stq=sb("stq",[P,2,6]); mvq=sb("mvq",[P,2,2]); vq=sb("vq",[P,2]); rq=sb("rq",[P,2]); nq=sb("nq",[P,2]); nq0=sb("nq0",[P,2])
        sto=sb("sto",[P,2,6]); mvo=sb("mvo",[P,2,2]); vo=sb("vo",[P,2]); ro=sb("ro",[P,2]); no=sb("no",[P,2]); no0=sb("no0",[P,2])
        z5=sb("z5",[P,2,512]); zg=sb("zg",[P,2,512]); zb=sb("zb",[P,512]); mq=sb("mq",[P,8]); e5=sb("e5",[P,2,512]); sq=sb("sq",[P,2,8]); eT=sb("eT",[P,512]); o5=sb("o5",[P,2,512]); z2=sb("z2",[P,2,512]); zT=sb("zT",[P,512])
        x5=sb("x5",[P,4,P]); x5T=sb("x5T",[P,NQ+1]); xm=sb("xm",[P,2,NQ]); xk=sb("xk",[P,NQ]); xr=sb("xr",[P,NQ]); kr6=sb("kr6",[P,NQ]); kact=sb("kact",[P,NQ]); sg=sb("sg",[P,NQ]); x6=sb("x6",[P,4,P])
        NW=len(names_w)+2+1
        def steps(e, body):
            for s in range(4): body(Step(None,s), True, s>=1, s>=2, s>=3, False)
            with e.Fori(0,3) as i:
                for u in range(4):
                    body(Step(i,4+u), True, True, True, True, True)
            for s in range(16,20): body(Step(None,s), False, s-1<NT, s-2<NT, s-3<NT, True)

        block=ctx.enter_context(nc.Block())
        class B:
            def __init__(s,i,k=0): s.i=i; s.k=k
            @property
            def n1(s): return s.i
            @property
            def n(s): return s.i if s.i is not None else s.k
        def loop(e,body):
            with e.Fori(0,NB) as i: body(B(i))
        bc=lambda ap,shape: ap.broadcast_to(shape)

        @block.sync
        def _(sp):
            for dst,src in ((wqkv_s[:],D['wqkv']),(wout_s[:],D['wout']),(bqkv_s[:],D['bqkv'].broadcast_to((P,384))),(bout_s[:],D['bout'].broadcast_to((P,P))),(xb[:],D['x'].rearrange("(t p) f -> p t f",p=P))):
                sp.dma_start(dst,src).then_inc(w_in.sem,16)
            sp.wait_ge(zeros.sem,6)
            def body(s, prep, smax, att1, att2, post):
                p=s.p
                if prep:
                    wait_apart(sp,proj,s,-1)
                    sp.dma_start(xT_s[:,p,:],D['xT'][:, bass.ds(s.n*P,P)]).then_inc(xt_in[p].sem,16)
                    wait_apart(sp,qkv_done,s,1)
                    wait_dma_apart(sp,v_in,s-2)
                    sp.dma_start(scr_v[p], qkv[:,p,256:384]).then_inc(v_out[p].sem,16)
                    wait_apart(sp,t2_done,s,1)
                    wait_dma_apart(sp,qk_in,s-2)
                    sp.dma_start(scr_t2[p], t2[:,p].rearrange("p a n -> p (a n)")).then_inc(t2_out[p].sem,16)
                    wait_dma_apart(sp,v_out,s)
                    wait_apart(sp,pv,s-3)
                    sp.dma_start(Vx[:,s.q,:,0:DH], scr_v[p].rearrange("(g t) (c e) -> g (t c) e",t=8,e=DH).rearrange("g q e -> q g e")).then_inc(v_in[p].sem,16)
                    wait_dma_apart(sp,t2_out,s)
                    sd=scr_t2[p].rearrange("(r s) (a n) -> a s r n",r=H4,a=2)
                    for dst,a,off,row in ((QX,0,0,0),(QX,0,0,24),(QX,0,8,48),(KX,1,0,0),(KX,1,8,24),(KX,1,0,48)):
                        sp.dma_start(dst[row:row+24,s.q], sd[a,off:off+24]).then_inc(qk_in[p].sem,16)
            steps(sp,body)
            sp.wait_ge(x1_cp.sem,NT); sp.wait_ge(x1T_sb.sem,NT)
            for n in names_w: sp.dma_start(wt[n][:],D[n]).then_inc(wB_in,16)
            sp.dma_start(rows[:],D['rows'].broadcast_to((P,nrow))).then_inc(wB_in,16)
            sp.dma_start(b2[:],D['b2']).then_inc(wB_in,16)
            sp.dma_start(vn[L:L+1,:],D['nv']).then_inc(wB_in,16)
            sp.wait_ge(zerosB,8)
            def body(b):
                WA(sp,b,'x5',0)
                sp.dma_start(ctx_s[:],D['ctxT'][bass.ds(b.n,1)].rearrange("o p l -> (o p) l")).then_inc(sems['ctx_in'],16)
                W(sp,b,'v_sb',1)
                for hh,k0,k1,c,r0 in ((0,0,77,0,0),(1,0,51,0,77),(1,51,77,1,0),(2,0,77,1,26),(3,0,25,1,103),(3,25,77,2,0)):
                    sp.dma_start(Vb[r0:r0+k1-k0,:,c,hh*DH:hh*DH+DH],v_s[k0:k1,:].rearrange("k (g h e) -> k g h e",g=4,h=4)[:,:,hh]).then_inc(sems['vb_in'],16)
                WA(sp,b,'x6',4)
                sp.dma_start(out[bass.ds(b.n,1)].rearrange("o (t p) f -> p (o t) f",p=P),x6[:]).then_inc(sems['out'],16)
            loop(sp,body)
            sp.wait_ge(sems['out'],16*NB)

        @block.gpsimd
        def _(g):
            n=[0]
            def c(ins):
                n[0]+=1; ins.then_inc(consts.sem,1); g.wait_ge(consts.sem,n[0])
            c(g.memset(idf[:],0.0))
            c(g.affine_select(out=idf[:],in_=idf[:],compare_op=ALU.not_equal,fill=1.0,base=0,pattern=[[-1,P]],channel_multiplier=1))
            c(g.tensor_copy(idb[:],idf[:]))
            c(g.memset(maskf[:],0.0))
            c(g.affine_select(out=maskf[:],in_=maskf[:],compare_op=ALU.is_ge,fill=BIG,base=0,pattern=[[1,P]],channel_multiplier=-1))
            c(g.tensor_copy(maskT[:],maskf[:]))
            c(g.memset(mhalf[:],-0.5))
            g.wait_ge(w_in.sem,80)
            g.tensor_tensor(xb[:],xb[:],bout_s[:].unsqueeze(1).broadcast_to((P,NT,P)),ALU.add).then_inc(xb_done.sem,1)
            def body(s, prep, smax, att1, att2, post):
                def select(t,j):
                    wait_apart(g,p_exp,t,[4,8,10,11][j])
                    v=Pr[:,j%2,:,0:P]
                    g.affine_select(out=v,in_=v,compare_op=ALU.is_ge,fill=0.0,base=0,pattern=[[0,H4],[1,P]],channel_multiplier=-1).then_inc(p_sel.sem,1)
                t=s-4
                if att2: select(s-3,2); select(s-3,3)
                if post:
                    wait_apart(g,mv_d,t,1)
                    g.tensor_scalar(vep[:],mv[:,1:2],1e-5,None,ALU.add).then_inc(vep_d.sem,1)
                    wait(g,vep_d,t,1)
                    g.tensor_tensor(rstd[:],vep[:],mhalf[:,0:1],ALU.pow).then_inc(rstd_d.sem,1)
                if att1: select(s-2,0); select(s-2,1)
                if post:
                    wait(g,x1_d,t,1)
                    dst = x1[:,bass.ds(t.n,1),:].rearrange("p o f -> p (o f)")
                    g.tensor_copy(dst,x1s[:]).then_inc(x1_cp.sem,1)
            steps(g,body)
            g.wait_ge(x1_cp.sem,NT); g.wait_ge(x1T_sb.sem,NT)
            n=[0]
            def c(ins):
                n[0]+=1; ins.then_inc(constsB,1); g.wait_ge(constsB,n[0])
            c(g.memset(blk8[:],1.0))
            c(g.affine_select(out=blk8[:],in_=blk8[:],compare_op=ALU.is_ge,fill=0.0,base=0,pattern=[[-DH,16],[0,DH]],channel_multiplier=1))
            c(g.affine_select(out=blk8[:],in_=blk8[:],compare_op=ALU.is_ge,fill=0.0,base=DH-1,pattern=[[DH,16],[0,DH]],channel_multiplier=-1))
            c(g.memset(obl[:],1.0))
            c(g.affine_select(out=obl[:],in_=obl[:],compare_op=ALU.is_ge,fill=0.0,base=0,pattern=[[128,3],[-L,4],[0,DH]],channel_multiplier=1))
            c(g.affine_select(out=obl[:],in_=obl[:],compare_op=ALU.is_ge,fill=0.0,base=L-1,pattern=[[-128,3],[L,4],[0,DH]],channel_multiplier=-1))
            c(g.memset(selp[:],0.0))
            c(g.affine_select(out=selp[:],in_=selp[:],compare_op=ALU.not_equal,fill=-1.0,base=0,pattern=[[-4,4],[-1,4],[0,L]],channel_multiplier=1))
            c(g.tensor_copy(sel[:],selp[:].rearrange("p g h k -> p g (h k)")))
            g.wait_ge(wB_in,16*NW); g.wait_ge(zerosB,8)
            def body(b):
                nb=b.n
                W(g,b,'xp',0)
                g.tensor_tensor(x1b[:],x1[:,bass.ds(nb*4,4),:],bc(row('bo',P).unsqueeze(1),(P,4,P)),ALU.add).then_inc(sems['x1b'],1)
                def rs(k):
                    WA(g,b,'mv',k)
                    g.tensor_scalar(vepb[:],mvb[:,:,1],1e-5,None,ALU.add).then_inc(sems['vep'],1)
                    W(g,b,'vep',k)
                    g.tensor_tensor(rstdb[:],vepb[:],mhalf[:],ALU.pow).then_inc(sems['rs'],1)
                rs(1); rs(2); rs(3); rs(4)
                def nrm(k,m,vv,r,n0,nn,pre_):
                    p=k%2
                    WA(g,b,m,k+1)
                    g.tensor_scalar(vv[:,p:p+1],mv_(m)[:,p,1:2],1e-5,None,ALU.add).then_inc(sems['v'+pre_],1)
                    W(g,b,'v'+pre_,k+1)
                    g.tensor_tensor(r[:,p:p+1],vv[:,p:p+1],mhalf[:,0:1],ALU.pow).then_inc(sems['r'+pre_],1)
                    WA(g,b,'r'+pre_,k+1)
                    g.tensor_tensor(n0[:,p:p+1],r[:,p:p+1],mv_(m)[:,p,0:1],ALU.mult).then_inc(sems['n'+pre_],1)
                mv_=lambda m: mvq if m=='mvq' else mvo
                def A(t): nrm(t,'mvq',vq,rq,nq,nq0,'q')
                def Z(t):
                    W(g,b,'z5',t+1); W(g,b,'zsub',t-1)
                    g.tensor_tensor(zg[:,t%2],z5[:,t%2],row('ln_q_g',512),ALU.mult).then_inc(sems['zg'],1)
                def O(t): nrm(t,'mvo',vo,ro,no,no0,'o')
                A(0);Z(0);A(1);Z(1);O(0);A(2);Z(2);O(1);A(3);Z(3);O(2);O(3)
                rs(5); rs(6)
            loop(g,body)

        @block.scalar
        def _(a):
            def body(s, prep, smax, att1, att2, post):
                if prep:
                    p=s.p
                    wait(a,qkv_done,s,1)
                    wait(a,t2_done,s-1)
                    src=qkv[:,p,0:256].rearrange("p (m e) -> p m e",e=DH)
                    dst=part[:,p].rearrange("p a c (s e) -> p (a c) s e",e=DH)
                    a.activation(dst[:,:,0:4:3],src.unsqueeze(2).broadcast_to((P,32,2,DH)),ACT.Copy).then_inc(part1.sem,1)
                def exps(t,lo,hi):
                    for n in range(lo,hi):
                        j,hs=UNITS_T[n]
                        wait(a,st_ready,t,n+1)
                        wait(a,pv,t,j-1)
                        N=P*(4-j)
                        k=len(hs)
                        a.activation(Pr[:,j%2,hs[0]:hs[0]+k,0:N], ps_T[(n+t.p)%2][:,0:k*N].rearrange("p (k n) -> p k n",k=k), ACT.Exp, scale=1/16.).then_inc(p_exp.sem,1)
                if att1:
                    t=s-2
                    wait(a,m_tr,t,1)
                    wait_dma(a,m_in,t-1)
                    a.activation(mT[:],ps_S[(11)%2][0:16,0:64].bitcast(BF16),ACT.Copy).then_inc(m_cp.sem,1)
                    wait(a,m_cp,t,1)
                    wait_dma(a,qk_in,t)
                    a.dma_start(QX[96:97,t.q].rearrange("o r (i n) -> o (r i) n",i=4),mT[:]).then_inc(m_in[t.p].sem,16)
                if att2: exps(s-3,8,11)
                t=s-4
                if post:
                    wait(a,aoT_ps,t,1)
                    a.activation(aoT[:],ps_post[:,0:P],ACT.Copy).then_inc(aoT_sb.sem,1)
                if att1: exps(s-2,0,8)
                if post:
                    wait(a,x1T_ps,t,1)
                    dst=x1T[:,bass.ds(t.n*P,P)]
                    a.activation(dst,ps_post[:,0:P],ACT.Copy).then_inc(x1T_sb.sem,1)
            steps(a,body)
            a.wait_ge(x1_cp.sem,NT); a.wait_ge(x1T_sb.sem,NT)
            def body(b):
                def act(out_,in_,f,name,**k): a.activation(out_,in_,f,**k).then_inc(sems[name],1)
                W(a,b,'p_kT',1); W(a,b,'kf',0)
                act(kT_s[:],bk[6][:,0:L],ACT.Identity,'kT_sb',bias=col('bk'))
                W(a,b,'p_qT',1); W(a,b,'p_T',0)
                act(qf[:],bk[6][:],ACT.Identity,'qf',bias=col('bq'))
                W(a,b,'p_m',1)
                act(mT2[:].rearrange("p (t n) -> p t n",t=4),bk[7][:,0:256].bitcast(BF16).rearrange("p (t n) -> p t n",t=4),ACT.Copy,'m_sb')
                for u in range(12):
                    c,gq=divmod(u,4); w=CW[c]
                    W(a,b,'p_T',u+1)
                    W(a,b,'p_pv',c-1)
                    act(Pr[0:w,c%2,gq],bk[u%4][0:w],ACT.Exp,'exp2',scale=DH**-0.5)
                W(a,b,'p_x2T',1)
                act(x2T[:],bk[7][:],ACT.Copy,'x2T')
                W(a,b,'esub',1)
                act(ge[:],es[:],ACT.Exp,'ge')
                def gelu(e):
                    for h in range(2):
                        u=2*e+h
                        W(a,b,'p_H',u+1)
                        W(a,b,'p_E',e-1)
                        act(Hb[:,e%2,h],bk[u%4][:],ACT.Gelu,'gelu',bias=col('b1',u))
                gelu(0); gelu(1)
                W(a,b,'p_GT',1)
                act(GT[:],bk[7][0:NE,:],ACT.Copy,'GT')
                for e in range(2,NE): gelu(e)
                W(a,b,'p_x3T',1)
                act(x3T[:],bk[7][:],ACT.Copy,'x3T')
                W(a,b,'p_q1',1)
                act(q1s[:],bk[3][:],ACT.Relu,'q1',bias=col('bq1'))
                for j in range(4):
                    W(a,b,'k5m',1); W(a,b,'p_kn',0)
                    a.activation(k5e[:,j],k5[:,j],ACT.Exp,bias=k5m[:,j:j+1],accum_out=k5s[:,j:j+1]).then_inc(sems['k5e'],1)
                W(a,b,'p_kn',1)
                act(kn[:],bk[2][0:L+1,:],ACT.Copy,'kn')
                W(a,b,'p_x4T',1)
                act(x4T[:],bk[7][:],ACT.Copy,'x4T')
                def z5f(t):
                    W(a,b,'nq',t+1); 
                    W(a,b,'p_q5',t+1); W(a,b,'zg',t-1)
                    act(z5[:,t%2],bk[4+t%2][:],ACT.Identity,'z5',scale=rq[:,t%2:t%2+1],bias=nq[:,t%2:t%2+1]) if 0 else act(z5[:,t%2],bk[4+t%2][:],ACT.Copy,'z5')
                def e5f(t):
                    W(a,b,'zsub',t+1); W(a,b,'p_eT',t-1); 
                    act(e5[:,t%2],zb[:],ACT.Exp,'e5')
                def eTf(t):
                    W(a,b,'p_eT',t+1); W(a,b,'p_o5',t)
                    act(eT[:],bk[6][:],ACT.Copy,'eT')
                def zTf(t):
                    W(a,b,'p_zT',t+1); W(a,b,'p_w5',t)
                    act(zT[:],bk[7][:],ACT.Copy,'zT')
                D5=dict(z=z5f,e=e5f,T=eTf,S=zTf)
                for s in "e0 T0 e1 T1 S0 e2 T2 S1 e3 T3 S2 S3".split(): D5[s[0]](int(s[1]))
                W(a,b,'p_x5T',1); W(a,b,'xk',0); W(a,b,'xr',0)
                act(x5T[:,1:NQ+1],bk[7][:],ACT.Copy,'x5T')
                W(a,b,'p_k6',1)
                act(kr6[:],bk[3][:],ACT.Relu,'kr6')
                W(a,b,'kr6',1)
                act(kact[:],kr6[:],ACT.Square,'kact')
                W(a,b,'p_r6',1)
                act(sg[:],bk[5][:],ACT.Exp,'sg',scale=-1.0)
            a.wait_ge(wB_in,16*NW); a.wait_ge(constsB,9)
            loop(a,body)

        @block.vector
        def _(v):
            n=[0]
            def c(ins):
                n[0]+=1; ins.then_inc(zeros.sem,1); v.wait_ge(zeros.sem,n[0])
            c(v.memset(KX[64:128],0.0)); c(v.memset(KX[96:97],-1.0)); c(v.memset(QX[64:128],0.0)) 
            c(v.memset(Vx[:],0.0)); c(v.memset(Vx[:,:,:,DH:DH+1],1.0)); c(v.memset(part[:],0.0))
            def body(s, prep, smax, att1, att2, post):
                if prep:
                    p=s.p
                    t=s
                    wait(v,proj,t,1)
                    wait_dma(v,v_out,s-2); wait(v,dprep,s-1)
                    v.tensor_tensor(qkv[:,p,:],ps_proj[:,0:384],bqkv_s[:],ALU.add).then_inc(qkv_done.sem,1)
                    dst=part[:,p].rearrange("p a c (s e) -> p (a c) s e",e=DH)
                    r1=res1[:,p].rearrange("p (m e) -> p m e",e=DH)
                    wait(v,qkv_done,t,1); wait(v,part1,t,1)
                    v.tensor_tensor(r1,qkv[:,p,0:256].rearrange("p (m e) -> p m e",e=DH),dst[:,:,0],ALU.subtract).then_inc(dprep.sem,1)
                    wait(v,dprep,t,1)
                    v.tensor_copy(dst[:,:,1],r1).then_inc(dprep.sem,1)
                    wait(v,dprep,t,2)
                    v.tensor_tensor(dst[:,:,2],r1,dst[:,:,1],ALU.subtract).then_inc(dprep.sem,1)
                    wait(v,dprep,t,3)
                    wait_dma(v,t2_out,s-2)
                    v.transpose(t2[:,p,0].rearrange("p (t c) -> p c t",c=C),part[:,p,0]).then_inc(dprep.sem,1)
                    v.transpose(t2[:,p,1].rearrange("p (t c) -> p c t",c=C),part[:,p,1]).then_inc(t2_done.sem,1)
                def maxes(t,p,lo,hi):
                    for n in range(lo,hi):
                        i,hs=UNITS_S[n]; k=len(hs); N=P*(i+1)
                        wait(v,s_ready,t,n+1)
                        if n==0: wait(v,m_tr,t-1)
                        v.tensor_reduce(mx[:,p].rearrange("p (r i) -> p r i",i=4)[:,hs[0]:hs[0]+k,i],ps_S[n%2][:,0:k*N].rearrange("p (k n) -> p k n",k=k),AX.X,ALU.max).then_inc(s_max.sem,1)
                if smax: maxes(s-1,(s-1).p,0,2)
                if post:
                    t=s-4; p=t.p
                    wait(v,pv,t,4); wait(v,ao_done,t)
                    v.transpose(OT[:].rearrange("p c t -> p c t"), ps_O[p][:].rearrange("p (t c) -> p c t",c=C)).then_inc(o_tr.sem,1)
                    wait(v,o_tr,t,1)
                    v.reciprocal(rc[:],OT[:,:,DH]).then_inc(o_rc.sem,1)
                    wait(v,o_rc,t,1); wait(v,aoT_ps,t)
                    v.tensor_tensor(ao[:],OT[:,:,0:DH],rc[:].unsqueeze(2).broadcast_to((P,C,DH)),ALU.mult).then_inc(ao_done.sem,1)
                if smax: maxes(s-1,(s-1).p,2,6)
                if post:
                    t=s-4
                    wait(v,y_ps,t,1)
                    if s.k<=7: v.wait_ge(xb_done.sem,1)
                    src=xb[:,bass.ds(t.n,1),:].rearrange("p o f -> p (o f)")
                    v.tensor_tensor(x1p[:],ps_post[:,P:2*P],src,ALU.add).then_inc(x1p_d.sem,1)
                    wait(v,x1p_d,t,1)
                    v.bn_stats(st[:],x1p[:]).then_inc(st_d.sem,1)
                    wait(v,rstd_d,t); wait_apart(v,st_d,t,1)
                    v.bn_aggr(mv[:],st[:]).then_inc(mv_d.sem,1)
                if smax: maxes(s-1,(s-1).p,6,9)
                if post:
                    t=s-4
                    wait(v,rstd_d,t,1); wait(v,x1T_ps,t); wait(v,x1_cp,t)
                    v.tensor_scalar(x1s[:],x1p[:],mv[:,0:1],rstd[:],ALU.subtract,ALU.mult).then_inc(x1_d.sem,1)
                if smax: maxes(s-1,(s-1).p,9,11)
            steps(v,body)
            v.wait_ge(x1_cp.sem,NT); v.wait_ge(x1T_sb.sem,NT)
            n=[0]
            def c(ins):
                n[0]+=1; ins.then_inc(zerosB,1); v.wait_ge(zerosB,n[0])
            c(v.memset(Vb[:],0.0)); c(v.memset(mx2[:],0.0)); c(v.memset(p8[:],3e38)); c(v.memset(cx[:],0.0)); c(v.memset(x5T[:,0:1],0.0)); c(v.memset(kvs[:,:,128:129],1.0))
            v.wait_ge(constsB,9); v.wait_ge(wB_in,16*NW)
            c(v.tensor_scalar(onemu[:],wt['cols'][:,CN['mu']:CN['mu']+2],-1.0,1.0,ALU.mult,ALU.add))
            c(v.tensor_copy(k5[:,:,L:L+1],bc(col('nk').unsqueeze(1),(P,4,1))))
            for j in range(4): v.tensor_scalar(wo5[:,j],wt['Wo5'][:,j*P:j*P+P],col('lng',j),None,ALU.mult).then_inc(pre,1)
            v.wait_ge(pre,5)
            v.tensor_copy(wb5[:],bk[0][:,0:P]).then_inc(pre,1)
            v.wait_ge(pre,6)
            link=[0]
            def body(b):
                def do(ins): link[0]+=1; ins.then_inc(sems['dv'],1)
                def settle(apart=False): (WA if apart else W)(v,b,'dv',link[0])
                def sg_(ins,name): ins.then_inc(sems[name],1)
                def stats(k):
                    W(v,b,'xp',k)
                    W(v,b,'vep',k-1)
                    for t in range(4): do(v.bn_stats(stb[:,t],xp[:,t]))
                    W(v,b,'rs',k-1); settle(True)
                    for t in range(4):
                        i=v.bn_aggr(mvb[:,t],stb[:,t])
                        if t<3: do(i)
                        else: sg_(i,'mv')
                def norm(k,dst,name):
                    W(v,b,'rs',k); W(v,b,'mv',k)
                    for t in range(4):
                        sg_(v.tensor_scalar(dst[:,t],xp[:,t],mvb[:,t,0:1],rstdb[:,t:t+1],ALU.subtract,ALU.mult),name)
                W(v,b,'p_v',1); W(v,b,'p_pv',0)
                sg_(v.tensor_tensor(v_s[:],bk[7][0:L,0:P],row('bv',P)[0:L],ALU.add),'v_sb')
                W(v,b,'kT_sb',1); W(v,b,'p_T',0)
                hk=lambda z: z.rearrange("p (h k) -> p h k",k=L)
                sg_(v.tensor_tensor(hk(Kf[:].rearrange("p g k -> p (g k)")),bc(kT_s[:].unsqueeze(1),(P,16,L)),bc(blk8[:,:,0:1],(P,16,L)),ALU.mult),'kf')
                W(v,b,'kf',1)
                sg_(v.tensor_copy(Khi[:],Kf[:].rearrange("p g k -> p (g k)")),'khi')
                W(v,b,'p_qT',1); W(v,b,'qf',1)
                sg_(v.tensor_scalar(qhi[:],bk[6][:],col('bq'),None,ALU.add),'qhi')
                for t in range(4):
                    for k,(h0,h1) in enumerate(((0,6),(6,12),(12,16))):
                        W(v,b,'p_S',3*t+k+1)
                        sg_(v.tensor_reduce(mx2[:,t,h0:h1],bk[3*(t%2)+k][:,0:(h1-h0)*L].rearrange("p (h k) -> p h k",k=L),AX.X,ALU.max),'mxd')
                W(v,b,'p_pv',3)
                sg_(v.reciprocal(rD[:],bk[5][:]),'rD')
                W(v,b,'rD',1); W(v,b,'p_y2',0)
                sg_(v.tensor_tensor(On[:],bk[4][:],rD[:],ALU.mult),'On')
                W(v,b,'p_y2',1); W(v,b,'x1b',1)
                sg_(v.tensor_tensor(xp[:],bk[6][:].rearrange("p (t f) -> p t f",t=4),x1b[:],ALU.add),'xp')
                stats(1); norm(1,x2,'x2')
                W(v,b,'p_lg',1)
                sg_(v.tensor_copy(lg[:],bk[6][:,0:64].rearrange("p (t e) -> p t e",t=4)[:,:,0:NE]),'lg')
                WA(v,b,'lg',1)
                for t in range(4): do(v.max(t8[:,t],lg[:,t]))
                settle()
                do(v.tensor_copy(p8[:,:,0:2],t8[:,:,0:2]))
                sg_(v.tensor_tensor(es[:],lg[:],bc(t8[:,:,0:1],(P,4,NE)),ALU.subtract),'esub')
                settle(True)
                for t in range(4): do(v.match_replace(lr[:,t],p8[:,t],lg[:,t],-3e38))
                settle()
                do(v.tensor_tensor(msk[:],lg[:],lr[:],ALU.not_equal))
                settle(); W(v,b,'ge',1)
                do(v.tensor_tensor(G[:],ge[:],msk[:],ALU.mult)); settle()
                do(v.tensor_reduce(gz[:],G[:],AX.X,ALU.add)); settle()
                do(v.reciprocal(gr[:],gz[:])); settle()
                sg_(v.tensor_tensor(G[:],G[:],bc(gr[:].unsqueeze(2),(P,4,NE)),ALU.mult),'G')
                W(v,b,'p_b2',1); W(v,b,'x2',4)
                sg_(v.tensor_tensor(acc[:],bk[6][:].rearrange("p (t f) -> p t f",t=4),x2[:],ALU.add),'accd')
                for e in range(NE):
                    W(v,b,'p_E',e+1); W(v,b,'accd',e+1)
                    for t in range(4):
                        if t<3:
                            if e>0: pass
                        i=v.scalar_tensor_tensor(out=acc[:,t],in0=bk[4+e%2][:,t*P:t*P+P],scalar=G[:,t,e:e+1],in1=acc[:,t],op0=ALU.mult,op1=ALU.add)
                        do(i) if t<3 else sg_(i,'accd')
                W(v,b,'accd',15); settle()
                do(v.tensor_scalar(acc[:],acc[:],-100.0,100.0,ALU.max,ALU.min)); settle()
                sg_(v.tensor_tensor(xp[:],acc[:],x2[:],ALU.add),'xp')
                stats(2); norm(2,x3,'x3')
                for k in range(2):
                    W(v,b,'p_kv',k+1)
                    r=row('bkv1',256)
                    src=bk[k][:].rearrange("p (t f) -> p t f",t=2)
                    do(v.tensor_tensor(kvs[:,2*k:2*k+2,0:128],src[:,:,128:256],bc(r[:,128:256].unsqueeze(1),(P,2,P)),ALU.add))
                    do(v.tensor_tensor(kvs[:,2*k:2*k+2,129:257],src[:,:,0:128],bc(r[:,0:128].unsqueeze(1),(P,2,P)),ALU.add))
                    settle()
                    sg_(v.tensor_scalar(kvs[:,2*k:2*k+2,129:257],kvs[:,2*k:2*k+2,129:257],0.0,None,ALU.max),'kvs')
                W(v,b,'p_kvm',1)
                sg_(v.tensor_tensor(kvm[:,0:128],bk[2][:,0:128],blk8[:].rearrange("p h e -> p (h e)"),ALU.mult),'kvm')
                sg_(v.tensor_scalar(kvm[:,128:144],blk8[:,:,0],bk[2][:,128:129],None,ALU.mult),'kvm')
                for k in range(2):
                    W(v,b,'p_ctx',k+1)
                    src=bk[4+k][:,0:288].rearrange("p (t f) -> p t f",t=2)
                    do(v.tensor_scalar(dn[:,2*k:2*k+2],src[:,:,128:144],1e-6,None,ALU.max)); settle()
                    do(v.reciprocal(dn[:,2*k:2*k+2],dn[:,2*k:2*k+2])); settle()
                    for t in range(2):
                        do(v.tensor_tensor(y4[:,2*k+t].rearrange("p (h e) -> p h e",e=DH),src[:,t,0:128].rearrange("p (h e) -> p h e",e=DH),bc(dn[:,2*k+t].unsqueeze(2),(P,16,DH)),ALU.mult))
                settle()
                sg_(v.tensor_tensor(xp[:],y4[:],x3[:],ALU.add),'xp')
                stats(3); norm(3,y4,'g4')
                W(v,b,'g4',4)
                do(v.tensor_tensor(y4[:],y4[:],bc(row('gamma',P).unsqueeze(1),(P,4,P)),ALU.mult)); settle()
                do(v.tensor_tensor(y4[:],y4[:],bc(row('beta',P).unsqueeze(1),(P,4,P)),ALU.add)); settle()
                sg_(v.tensor_tensor(xp[:],y4[:],x3[:],ALU.add),'xp')
                stats(4); norm(4,x4,'x4')
                W(v,b,'p_k5',1); W(v,b,'k5e',0)
                sg_(v.tensor_copy(k5[:,:,0:L],bk[0][:,0:4*L].rearrange("p (j l) -> p j l",j=4)),'k5')
                W(v,b,'k5',1)
                do(v.tensor_reduce(k5m[:],k5[:],AX.X,ALU.max)); settle()
                sg_(v.tensor_scalar(k5m[:],k5m[:],-1.0,None,ALU.mult),'k5m')
                W(v,b,'p_v5',1)
                sg_(v.tensor_copy(vn[0:L,:],bk[1][0:L,:]),'v5')
                W(v,b,'k5e',4)
                sg_(v.reciprocal(k5s[:],k5s[:]),'k5s')
                W(v,b,'k5s',1)
                for j in range(4): sg_(v.tensor_scalar(k5e[:,j],k5e[:,j],k5s[:,j:j+1],8.0,ALU.mult,ALU.mult),'k5n')
                W(v,b,'p_cx',1)
                for h in range(2):
                    s=slice(64*h,64*h+64)
                    sg_(v.tensor_copy(cx[s,:,64*h:64*h+64],bk[3][s,:].rearrange("p (j e) -> p j e",j=4)[:,:,64*h:64*h+64]),'cx')
                def Q(t):
                    p=t%2
                    W(v,b,'p_q5',t+1); W(v,b,'nq',t-1)
                    do(v.bn_stats(stq[:,p],bk[4+p][:])); settle(True)
                    sg_(v.bn_aggr(mvq[:,p],stq[:,p]),'mvq')
                def R(t):
                    p=t%2
                    W(v,b,'rq',t+1); W(v,b,'zg',t-1); W(v,b,'mvq',t+1)
                    sg_(v.tensor_scalar(z5[:,p],bk[4+p][:],mvq[:,p,0:1],rq[:,p:p+1],ALU.subtract,ALU.mult),'z5')
                def M(t):
                    p=t%2
                    W(v,b,'zg',t+1); W(v,b,'e5',t)
                    do(v.tensor_tensor(zb[:],zg[:,p],row('ln_q_b',512),ALU.add)); settle()
                    zz=zb[:].rearrange("p (h d) -> p h d",h=8)
                    do(v.tensor_reduce(mq[:],zz,AX.X,ALU.max)); settle()
                    sg_(v.tensor_tensor(zz,zz,bc(mq[:].unsqueeze(2),(P,8,64)),ALU.subtract),'zsub')
                def U(t):
                    p=t%2
                    W(v,b,'e5',t+1)
                    do(v.tensor_reduce(sq[:,p],e5[:,p].rearrange("p (h d) -> p h d",h=8),AX.X,ALU.add)); settle()
                    do(v.reciprocal(sq[:,p],sq[:,p])); settle()
                def OO(t):
                    p=t%2
                    W(v,b,'p_o5',t+1); W(v,b,'z2',t-1)
                    sg_(v.tensor_tensor(o5[:,p].rearrange("p (h d) -> p h d",h=8),bk[t%2][:].rearrange("p (h d) -> p h d",h=8),bc(sq[:,p].unsqueeze(2),(P,8,64)),ALU.mult),'o5')
                    W(v,b,'o5',t+1)
                    do(v.bn_stats(sto[:,p],o5[:,p])); W(v,b,'no',t-1); settle(True)
                    sg_(v.bn_aggr(mvo[:,p],sto[:,p]),'mvo')
                def X(t):
                    p=t%2
                    W(v,b,'ro',t+1); W(v,b,'p_zT',t-1); W(v,b,'mvo',t+1)
                    sg_(v.tensor_scalar(z2[:,p],o5[:,p],mvo[:,p,0:1],ro[:,p:p+1],ALU.subtract,ALU.mult),'z2')
                D5=dict(Q=Q,R=R,M=M,U=U,O=OO,X=X)
                for s in "Q0 R0 M0 Q1 R1 U0 M1 O0 X0 Q2 R2 U1 M2 O1 X1 Q3 R3 U2 M3 O2 X2 U3 O3 X3".split(): D5[s[0]](int(s[1]))
                W(v,b,'x4',4)
                do(v.tensor_tensor(y4[:],x4[:],bc(wb5[:].unsqueeze(1),(P,4,P)),ALU.add)); settle()
                W(v,b,'p_w5',4)
                sg_(v.tensor_tensor(xp[:],bk[2][:].rearrange("p (t f) -> p t f",t=4),y4[:],ALU.add),'xp')
                stats(5); norm(5,x5,'x5')
                W(v,b,'x5T',1)
                sg_(v.tensor_scalar(xm[:,0],x5T[:,1:NQ+1],col('mu',0),None,ALU.mult),'xm')
                sg_(v.tensor_scalar(xm[:,1],x5T[:,1:NQ+1],col('mu',1),None,ALU.mult),'xm')
                W(v,b,'xm',2)
                W(v,b,'p_k6',0)
                sg_(v.scalar_tensor_tensor(out=xk[:],in0=x5T[:,0:NQ],scalar=onemu[:,1:2],in1=xm[:,1],op0=ALU.mult,op1=ALU.add),'xk')
                W(v,b,'p_r6',0)
                sg_(v.scalar_tensor_tensor(out=xr[:],in0=x5T[:,0:NQ],scalar=onemu[:,0:1],in1=xm[:,0],op0=ALU.mult,op1=ALU.add),'xr')
                W(v,b,'sg',1)
                do(v.tensor_scalar(sg[:],sg[:],1.0,None,ALU.add)); settle()
                do(v.reciprocal(sg[:],sg[:])); settle()
                W(v,b,'p_v6',1)
                do(v.tensor_tensor(y4[:].rearrange("p t f -> p (t f)"),bk[4][:],sg[:],ALU.mult)); settle(); W(v,b,'x5',4)
                sg_(v.tensor_tensor(xp[:],y4[:],x5[:],ALU.add),'xp')
                stats(6); 
                W(v,b,'out',0)
                norm(6,x6,'x6')
                if link[0]!=PER['dv']: raise SystemExit(f"dv = {link[0]}")
            loop(v,body)

        @block.tensor
        def _(pe):
            pe.wait_ge(consts.sem,7); pe.wait_ge(w_in.sem,80)
            def project(t):
                wait_dma(pe,xt_in,t)
                wait(pe,qkv_done,t)
                pe.matmul(ps_proj[:,0:384],xT_s[:,t.p],wqkv_s[:],start=True,stop=True).then_inc(proj.sem,1)
            def body(s, prep, smax, att1, att2, post):
                def S(lo,hi):
                    if not smax: return
                    t=s-1; p=(s-1).p
                    for n in range(lo,hi):
                        i,hs=UNITS_S[n]; N=P*(i+1)
                        if n==0: wait_dma(pe,qk_in,t); wait_dma(pe,v_in,t)
                        wait(pe,s_max,t,n-1)
                        if n==1: wait(pe,m_cp,t)
                        for k,r in enumerate(hs):
                            pe.matmul(ps_S[n%2][:,k*N:(k+1)*N],QX[0:96,t.q,r,P*i:P*i+P],KX[0:96,t.q,r,0:N],start=True,stop=False)
                            l=pe.matmul(ps_S[n%2][:,k*N+P*i:(k+1)*N],maskT[:],idb[:],start=False,stop=True)
                        l.then_inc(s_ready.sem,1)
                def T(t,*units):
                    for n in units:
                        j,hs=UNITS_T[n]; N=P*(4-j)
                        if n==0: wait_dma(pe,m_in,t)
                        wait(pe,p_exp,t,n-1)
                        for k,r in enumerate(hs):
                            l=pe.matmul(ps_T[(n+t.p)%2][:,k*N:(k+1)*N],KX[0:97,t.q,r,P*j:P*j+P],QX[0:97,t.q,r,P*j:NP],start=True,stop=True)
                        l.then_inc(st_ready.sem,1)
                def PV(t,j):
                    p=t.p
                    N=P*(4-j)
                    wait(pe,p_sel,t,j+1)
                    if j==0: wait(pe,o_tr,t-1)
                    for r in range(H4):
                        l=pe.matmul(ps_O[p][32*r:32*r+32,P*j:NP],Vx[:,t.q,4*r+j,:],Pr[:,j%2,r,0:N],start=(j==0),stop=(j==3))
                    l.then_inc(pv.sem,1)
                if prep: project(s)
                if att1:
                    t=s-2
                    wait(pe,s_max,t,11)
                    pe.transpose(ps_S[1][0:16,0:64].bitcast(BF16),mx[:,t.p],idb[:]).then_inc(m_tr.sem,1)
                S(0,2)
                if att2:
                    T(s-3,8,9); PV(s-3,1); T(s-3,10)
                S(2,3)
                if att2: PV(s-3,2)
                S(3,4)
                if att2: PV(s-3,3)
                t=s-4
                if post:
                    wait(pe,ao_done,t,1); wait(pe,x1T_sb,t)
                    pe.transpose(ps_post[:,0:P],ao[:].rearrange("p c e -> p (c e)"),idf[:]).then_inc(aoT_ps.sem,1)
                S(4,5)
                if att1: T(s-2,0,1)
                S(5,6)
                if att1: T(s-2,2)
                if post:
                    wait(pe,aoT_sb,t,1)
                    pe.matmul(ps_post[:,P:2*P],aoT[:],wout_s[:],start=True,stop=True).then_inc(y_ps.sem,1)
                S(6,7)
                if att1: T(s-2,3)
                S(7,8)
                if att1: T(s-2,4,5)
                S(8,9)
                if att1: T(s-2,6)
                S(9,10)
                if att1: T(s-2,7)
                S(10,11)
                if att1: PV(s-2,0)
                if post:
                    wait(pe,x1_d,t,1)
                    pe.transpose(ps_post[:,0:P],x1s[:],idf[:]).then_inc(x1T_ps.sem,1)
            steps(pe,body)
            pe.wait_ge(x1_cp.sem,NT); pe.wait_ge(x1T_sb.sem,NT)
            pe.wait_ge(wB_in,16*NW); pe.wait_ge(constsB,9); pe.wait_ge(zerosB,8); pe.wait_ge(pre,4)
            for j in range(4): l=pe.matmul(bk[0][:,0:P],bc(col('lnb',j),(P,P)),wt['Wo5'][:,j*P:j*P+P],start=j==0,stop=j==3)
            l.then_inc(pre,1)
            pe.wait_ge(pre,6)
            def body(b):
                mm=lambda o,l,r,s=True,e=True: pe.matmul(o,l,r,start=s,stop=e)
                def sg_(ins,name): ins.then_inc(sems[name],1)
                W(pe,b,'ctx_in',16)
                W(pe,b,'x5T',0)
                sg_(mm(bk[6][:,0:L],wt['wk'][:],ctx_s[:]),'p_kT')
                sg_(mm(bk[7][0:L,0:P],ctx_s[:],wt['wv'][:]),'p_v')
                W(pe,b,'kT_sb',1)
                sg_(mm(bk[6][:],wt['wq'][:],x1T[:,bass.ds(b.n*NQ,NQ)]),'p_qT')
                W(pe,b,'khi',1); W(pe,b,'qhi',1); W(pe,b,'x6',0)
                for t in range(4):
                    W(pe,b,'mxd',3*(t-1)) if t>=2 else None
                    for k,(h0,h1) in enumerate(((0,6),(6,12),(12,16))):
                        sg_(mm(bk[3*(t%2)+k][:,0:(h1-h0)*L],qhi[:,t*P:t*P+P],Khi[:,h0*L:h1*L]),'p_S')
                W(pe,b,'mxd',12); W(pe,b,'v_sb',1)
                m7=bk[7][:,0:256].bitcast(BF16)
                for t in range(4): l=pe.transpose(m7[:,t*P:t*P+P],mx2[:,t],idb[:])
                sg_(l,'p_m')
                W(pe,b,'m_sb',1); W(pe,b,'qf',1); W(pe,b,'kf',1)
                def T(u):
                    c,gq=divmod(u,4); w=CW[c]
                    W(pe,b,'exp2',u-3) if u>3 else None
                    s=slice(c*128,c*128+w)
                    mm(bk[u%4][0:w],Kf[:,gq,s],qf[:],True,False)
                    sg_(mm(bk[u%4][0:w],sel[:,gq,s],mT2[:],False,True),'p_T')
                def PV(c):
                    w=CW[c]
                    WA(pe,b,'exp2',4*c+4)
                    if c==0: W(pe,b,'vb_in',96)
                    for gq in range(4): mm(bk[4][32*gq:32*gq+32],Vb[0:w,gq,c],Pr[0:w,c%2,gq],c==0,c==2)
                    for gq in range(4): l=mm(bk[5][32*gq:32*gq+32],obl[0:w,c].rearrange("p h e -> p (h e)"),Pr[0:w,c%2,gq],c==0,c==2)
                    sg_(l,'p_pv')
                for u in range(8): T(u)
                PV(0)
                for u in range(8,12): T(u)
                PV(1); PV(2)
                W(pe,b,'On',1)
                for t in range(4): l=mm(bk[6][:,t*P:t*P+P],On[:,t*P:t*P+P],wt['wo'][:])
                sg_(l,'p_y2')
                def XT(src,name,pn,extra=None):
                    for t in range(4):
                        W(pe,b,name,t+1)
                        l=pe.transpose(bk[7][:,t*P:t*P+P],src[:,t],idf[:])
                    sg_(l,pn)
                XT(x2,'x2','p_x2T')
                W(pe,b,'x2T',1)
                for t in range(4): l=mm(bk[6][:,t*16:t*16+NE],x2T[:,t*P:t*P+P],wt['gate'][:])
                sg_(l,'p_lg')
                def H(e):
                    for h in range(2):
                        u=2*e+h
                        W(pe,b,'gelu',u-3) if u>3 else None
                        sg_(mm(bk[u%4][:],wt['w1'][:,e*F+h*P:e*F+h*P+P],x2T[:]),'p_H')
                def E(e):
                    W(pe,b,'gelu',2*e+2); W(pe,b,'accd',e) if e>=2 else None
                    for t in range(4):
                        for h in range(2):
                            l=mm(bk[4+e%2][:,t*P:t*P+P],Hb[:,e%2,h,t*P:t*P+P],wt['w2'][:,(2*e+h)*P:(2*e+h+1)*P],h==0,h==1)
                    sg_(l,'p_E')
                H(0);H(1);E(0)
                W(pe,b,'G',1)
                for t in range(4): l=pe.transpose(bk[7][0:NE,t*P:t*P+P],G[:,t],idf[:])
                sg_(l,'p_GT')
                H(2);E(1)
                W(pe,b,'GT',1)
                for t in range(4): l=mm(bk[6][:,t*P:t*P+P],GT[:,t*P:t*P+P],b2[:])
                sg_(l,'p_b2')
                for e in range(3,NE): H(e); E(e-1)
                E(NE-1)
                XT(x3,'x3','p_x3T')
                W(pe,b,'x3T',1)
                for t in range(4):
                    l=mm(bk[t//2][:,(t%2)*256:(t%2)*256+256],x3T[:,t*P:t*P+P],wt['wkv1'][:])
                    if t%2: sg_(l,'p_kv')
                sg_(mm(bk[3][:],wt['wq1'][:],x3T[:]),'p_q1')
                W(pe,b,'kvs',2)
                for t in range(4): l=mm(bk[2][:,0:129],kvs[:,t,129:257],kvs[:,t,0:129],t==0,t==3)
                sg_(l,'p_kvm')
                W(pe,b,'kvm',2); W(pe,b,'q1',1)
                for t in range(4):
                    l=mm(bk[4+t//2][:,(t%2)*144:(t%2)*144+144],q1s[:,t*P:t*P+P],kvm[:])
                    if t%2: sg_(l,'p_ctx')
                for j in range(4): l=mm(bk[0][:,j*L:(j+1)*L],wt['Wk5'][:,j*P:j*P+P],ctx_s[:])
                sg_(l,'p_k5')
                sg_(mm(bk[1][0:L,:],ctx_s[:],wt['Wv5'][:]),'p_v5')
                XT(x4,'x4','p_x4T')
                W(pe,b,'k5n',4)
                for j in range(4): l=pe.transpose(bk[2][0:L+1,j*P:j*P+P],k5e[:,j],idf[:])
                sg_(l,'p_kn')
                W(pe,b,'kn',1); W(pe,b,'v5',1)
                for j in range(4): l=mm(bk[3][:,j*P:j*P+P],kn[:,j*P:j*P+P],vn[:,j*P:j*P+P])
                sg_(l,'p_cx')
                W(pe,b,'x4T',1)
                def q(t):
                    W(pe,b,'z5',t-1) if t>=2 else None
                    sg_(mm(bk[4+t%2][:],x4T[:,t*P:t*P+P],wt['Wq5'][:]),'p_q5')
                def a(t):
                    W(pe,b,'e5',t+1); W(pe,b,'eT',t)
                    for j in range(4): l=pe.transpose(bk[6][:,j*P:j*P+P],e5[:,t%2,j*P:j*P+P],idf[:])
                    sg_(l,'p_eT')
                def o(t):
                    W(pe,b,'eT',t+1); W(pe,b,'o5',t-1) if t>=2 else None
                    if t==0: W(pe,b,'cx',2)
                    for j in range(4): l=mm(bk[t%2][:,j*P:j*P+P],eT[:,j*P:j*P+P],cx[:,j])
                    sg_(l,'p_o5')
                def z(t):
                    W(pe,b,'z2',t+1); W(pe,b,'zT',t)
                    for j in range(4): l=pe.transpose(bk[7][:,j*P:j*P+P],z2[:,t%2,j*P:j*P+P],idf[:])
                    sg_(l,'p_zT')
                def w(t):
                    W(pe,b,'zT',t+1)
                    for j in range(4): l=mm(bk[2][:,t*P:t*P+P],zT[:,j*P:j*P+P],wo5[:,j],j==0,j==3)
                    sg_(l,'p_w5')
                D5=dict(q=q,a=a,o=o,z=z,w=w)
                for s in "q0 q1 a0 o0 q2 a1 o1 z0 w0 q3 a2 o2 z1 w1 a3 o3 z2 w2 z3 w3".split(): D5[s[0]](int(s[1]))
                XT(x5,'x5','p_x5T')
                W(pe,b,'xk',1)
                sg_(mm(bk[3][:],wt['Wk6'][:],xk[:]),'p_k6')
                W(pe,b,'xr',1)
                for t in range(4): l=mm(bk[5][:,t*P:t*P+P],xr[:,t*P:t*P+P],wt['Wr'][:])
                sg_(l,'p_r6')
                W(pe,b,'kact',1)
                for t in range(4): l=mm(bk[4][:,t*P:t*P+P],kact[:,t*P:t*P+P],wt['Wv6'][:])
                sg_(l,'p_v6')
            loop(pe,body)

def host(I):
    T=lambda a: np.ascontiguousarray(a.T)
    D={}
    x=I['x'].reshape(NT*P,P)
    D['x']=x; D['xT']=T(x)
    D['wqkv']=np.ascontiguousarray(I['L0_attn_W_qkv'].reshape(P,C,3,DH).transpose(0,2,1,3).reshape(P,3*P))
    D['bqkv']=np.ascontiguousarray(I['L0_attn_b_qkv'].reshape(C,3,DH).transpose(1,0,2).reshape(1,3*P))
    D['wout']=I['L0_attn_W_out']; D['bout']=I['L0_attn_b_out'].reshape(1,P)
    D['ctxT']=np.ascontiguousarray(I['ctx_1024'].transpose(0,2,1))
    D['wq']=T(I['L0_xattn_wq']);D['wk']=T(I['L0_xattn_wk']);D['wv']=T(I['L0_xattn_wv']);D['wo']=T(I['L0_xattn_wo'])
    D['gate']=T(I['L0_ffn_gate_w'])
    D['w1']=np.ascontiguousarray(I['L0_ffn_w1'].transpose(1,0,2).reshape(P,NE*F))
    D['w2']=np.ascontiguousarray(I['L0_ffn_w2'].reshape(NE*2,P,P).transpose(1,0,2).reshape(P,NE*2*P))
    D['wkv1']=np.ascontiguousarray(np.concatenate([I['L1_attn_Wk'].T,I['L1_attn_Wv'].T],1)); D['wq1']=T(I['L1_attn_Wq'])
    D['Wq5']=I['L1_xattn_Wq']; D['Wk5']=np.ascontiguousarray(I['L1_xattn_Wkv'][:,:512]); D['Wv5']=np.ascontiguousarray(I['L1_xattn_Wkv'][:,512:])
    D['Wo5']=np.ascontiguousarray(I['L1_xattn_Wout'].reshape(4,P,P).transpose(1,0,2).reshape(P,512))
    D['Wr']=T(I['L1_ffn_W_r']);D['Wk6']=T(I['L1_ffn_W_k']);D['Wv6']=T(I['L1_ffn_W_v'])
    cols=[('bq',I['L0_xattn_bq'][:,None]),('bk',I['L0_xattn_bk'][:,None]),('bq1',I['L1_attn_bq'][:,None]),('b1',I['L0_ffn_b1'].reshape(NE*2,P).T),
      ('lng',I['L1_xattn_ln_out_g'].reshape(4,P).T),('lnb',I['L1_xattn_ln_out_b'].reshape(4,P).T),('mu',np.stack([I['L1_ffn_mu_r'],I['L1_ffn_mu_k']],1)),('nk',np.tile(I['L1_xattn_null_kv'][0],2)[:,None])]
    CN={};o=0
    for n,a in cols: CN[n]=o;o+=a.shape[1]
    D['cols']=np.ascontiguousarray(np.concatenate([a for _,a in cols],1))
    rows=[('bv',I['L0_xattn_bv']),('bo',I['L0_xattn_bo']),('bkv1',np.concatenate([I['L1_attn_bk'],I['L1_attn_bv']])),('gamma',I['L1_attn_gamma']),('beta',I['L1_attn_beta']),('ln_q_g',I['L1_xattn_ln_q_g']),('ln_q_b',I['L1_xattn_ln_q_b'])]
    RN={};o=0
    for n,a in rows: RN[n]=o;o+=a.shape[0]
    D['rows']=np.ascontiguousarray(np.concatenate([a for _,a in rows])[None])
    D['b2']=I['L0_ffn_b2']
    nk,nv=I['L1_xattn_null_kv']
    D['nv']=np.ascontiguousarray(np.tile(nv,8)[None])
    return D,CN,RN

def kernel(**inputs):
    import concourse.bacc as bacc
    from concourse.bass_utils import run_bass_kernel_spmd
    D,CN,RN=host({k:np.asarray(v) for k,v in inputs.items()})
    nc=bacc.Bacc("TRN2", target_bir_lowering=False, num_devices=1)
    arrays={"in_"+k:np.ascontiguousarray(v) for k,v in D.items()}
    aps={k:nc.dram_tensor("in_"+k, arrays["in_"+k].shape, mybir.dt.from_np(arrays["in_"+k].dtype), kind="ExternalInput").ap() for k in D}
    out=nc.dram_tensor("out_x", (NB,NQ,P), F32, kind="ExternalOutput").ap()
    build(nc, CN, RN, out, aps)
    r=run_bass_kernel_spmd(nc, [arrays], core_ids=[0])
    return r.results[0]["out_x"]
```

```python
from contextlib import ExitStack

import numpy as np
import concourse.bass as bass
from concourse import mybir
from concourse.alu_op_type import AluOpType as ALU

ACT=mybir.ActivationFunctionType
AX=mybir.AxisListType
F32=mybir.dt.float32
BF16=mybir.dt.bfloat16
P=128
NT=16
H4=4
C=16
DH=8
NP=512
BIG=-1e30
NB=4
L=77
LG=4*L
NE=14
F=256
NQ=512


class Sem:
    def __init__(self, sem, per): self.sem, self.per = sem, per
    def upto(self, t, n=0):
        return t * self.per + n

class Step:
    def __init__(self, i, k): self.i, self.k = i, k
    def __sub__(self, d): return Step(self.i, self.k - d)
    def __add__(self, d): return Step(self.i, self.k + d)
    @property
    def n(self): return self.k if self.i is None else self.i * 4 + self.k
    @property
    def half(self): return self.k // 2 if self.i is None else self.i * 2 + self.k // 2
    @property
    def p(self): return self.k % 2
    @property
    def q(self): return self.k % 4
    def first(self, n): return self.i is None and self.k < n

def wait(e, s, t, n=0):
    v = s.upto(t.n, n)
    if isinstance(v, int) and v <= 0:
        return
    e.wait_ge(s.sem, v)

def wait_apart(e, s, t, n=0):
    wait(e, s, t, n)
    if t.i is not None:
        e.nop(nofuse=True)

def wait_dma(e, s, t):
    if t.first(0): return
    s = s[t.p]
    e.wait_ge(s.sem, (t.half + 1) * s.per)

def wait_dma_apart(e, s, t):
    wait_dma(e, s, t)
    if t.i is not None:
        e.nop(nofuse=True)

UNITS_S = [(0,[0,1,2,3]),(1,[0,1]),(1,[2,3])]+[(2,[r]) for r in range(4)]+[(3,[r]) for r in range(4)]
UNITS_T = [(0,[r]) for r in range(4)]+[(1,[r]) for r in range(4)]+[(2,[0,1]),(2,[2,3]),(3,[0,1,2,3])]

PE_STEP = [("project", 0, 1), ("T", 7, 4), ("S", 0, 2), ("maxima", 0, 3), ("PV", 0, 4), ("T", 8, 4), ("T", 9, 4), ("S", 1, 2), ("PV", 1, 4), ("T", 10, 4),
           ("S", 2, 2), ("T", 0, 3), ("PV", 2, 4), ("S", 3, 2), ("out_turn", 0, 5), ("PV", 3, 4), ("S", 4, 2), ("T", 1, 3), ("S", 5, 2), ("out", 0, 5),
           ("S", 6, 2), ("T", 2, 3), ("S", 7, 2), ("T", 3, 3), ("T", 4, 3), ("S", 8, 2), ("S", 9, 2), ("T", 5, 3), ("T", 6, 3), ("S", 10, 2), ("x1_turn", 0, 5)]
DVE_STEP = [("bias", 0, 1), ("max", 0, 2), ("parts", 1, 1), ("parts", 2, 1), ("parts", 3, 1), ("heads", 0, 1), ("heads", 1, 1), ("out_turn", 0, 5),
            ("max", 1, 2), ("norm", 0, 5), ("max", 2, 2), ("max", 3, 2), ("max", 4, 2), ("max", 5, 2), ("sum", 0, 5), ("max", 6, 2), ("max", 7, 2),
            ("max", 8, 2), ("x1", 0, 5), ("max", 9, 2), ("max", 10, 2)]
ACT_STEP = [("exp", 7, 4), ("parts", 0, 1), ("maxima", 0, 3), ("exp", 8, 4), ("exp", 9, 4), ("exp", 10, 4), ("out_turn", 0, 5), ("exp", 0, 3), ("exp", 1, 3),
            ("exp", 2, 3), ("x_copy", 0, 0), ("exp", 3, 3), ("exp", 4, 3), ("exp", 5, 3), ("exp", 6, 3), ("x1_turn", 0, 5)]
POOL_STEP = [("variance", 0, 5), ("select", 0, 3), ("keep", 0, 5), ("select", 1, 3), ("x_bias", 0, 2), ("select", 2, 3), ("select", 3, 3)]


def tile(s, lag):
    t = s - lag
    return None if t.i is None and not 0 <= t.k < NT else t


def steps(e, order, part):
    def step(s):
        for what, n, lag in order:
            t = tile(s, lag)
            if t is not None:
                part(what, n, t)
    for s in range(8): step(Step(None, s))
    with e.Fori(0, 2) as i:
        for u in range(4): step(Step(i, 8 + u))
    for s in range(16, 21): step(Step(None, s))

CW=[128,128,52]
PER_BATCH = dict(
    v_blocks_in=96, x1_bias_done=1, kT_done=1, v_done=1, k_spread=1, k_bf16_done=1, q_done=1, q_bf16_done=1, bound_done=12, boundT_done=1,
    probs_done=12, heads_done=2, norm_in=1, norm_stats=1, norm_scale=1, x2_done=4, x2T_done=1, logits_shifted=1, logits_exp=1, gates_done=1,
    gatesT_done=1, hidden_done=28, expert_added=56, moe_begun=1, x3_done=4, x3T_done=1, kv_done=2, kv_sum_done=2, q1_done=1, x4_done=4,
    x4T_done=1, k5_normed=4, k5_max_done=1, k5_exp_done=4, k5T_done=1, v5_done=1, context_done=2, q5_stats=4, q5_normed=4, q5_less_max=4,
    q5_exp_done=4, q5T_done=4, o5_done=4, o5_normed=4, o5T_done=4, x5_done=4, x5T_done=1, xk_done=1, xr_done=1, k6_relu=1, k6_squared=1,
    r6_sigmoid=1, x6_done=4, q5_scale=4, o5_stats=4, o5_scale=4, kT_ready=1, v_ready=1, q_ready=1, bound_ready=12, bound_turned=1,
    scores_ready=12, values_ready=3, cross_ready=1, x2T_ready=1, logits_ready=1, hidden_ready=28, expert_ready=14, gates_turned=1,
    gate_bias_ready=1, x3T_ready=1, kv_ready=2, q1_ready=1, kv_sum_ready=1, linear_ready=2, x4T_ready=1, k5_ready=1, v5_ready=1, k5_turned=1,
    context_ready=1, q5_ready=4, q5_turned=4, o5_ready=4, o5_turned=4, second_ready=4, x5T_ready=1, k6_ready=1, r6_ready=1, v6_ready=1,
    out_written=16, dve_own=0, x5_mixed=2, pool_own=0, x3_beta_done=1, q5_summed=4, gated_done=1)
S_BANKS=(3,4,6)
T_BANKS=(3,4,7)
CROSS = [("keys", 0, 4), ("query", 0, 2), ("bound", 0, 1), ("bound", 1, 0), ("bound", 2, 0), ("bound", 3, 3), ("bound_turn", 0, 3), ("scores", 0, 0),
         ("scores", 1, 0), ("values", 0, 0), ("scores", 2, 0), ("values", 1, 1), ("scores", 3, 1), ("values", 2, 3), ("cross_out", 0, 2),
         ("cross_turn", 0, 3), ("gate", 0, 6), ("gate_turn", 0, 1), ("gate_bias", 0, 0)]
REST = [("moe_out", 0, 8), ("moe_turn", 0, 4), ("linear", 0, 1), ("linear_sum", 0, 2), ("linear_out", 0, 4), ("context", 0, 5), ("linear_norm", 0, 6),
        ("context_turn", 0, 0), ("linear_turn", 0, 2), ("context_out", 0, 0), ("q", 0, 4), ("m", 0, 0), ("q", 1, 0), ("a", 0, 0), ("m", 1, 0),
        ("q", 2, 0), ("o", 0, 1), ("q", 3, 2), ("a", 1, 2), ("z", 0, 0), ("m", 2, 1), ("o", 1, 1), ("a", 2, 0), ("w", 0, 0), ("z", 1, 0), ("m", 3, 0),
        ("o", 2, 3), ("a", 3, 0), ("w", 1, 0), ("z", 2, 0), ("o", 3, 2), ("w", 2, 0), ("z", 3, 1), ("w", 3, 3), ("second_out", 0, 3),
        ("second_turn", 0, 6), ("ffn_in", 0, 3), ("ffn_out", 0, 1), ("ffn_norm", 0, 5)]
EXPERT = [x for e in range(NE + 1) for x in ([("up", e)] if e < NE else []) + ([("down", e - 1)] if e else [])]


def beside(long, b_experts):
    if b_experts is None:
        return [(s, b, k) for s, b, k, _ in long]
    total, so_far, done, order = sum(x[3] for x in long), 0, 0, []
    for s, b, k, weight in long:
        order.append((s, b, k))
        so_far += weight
        while done < len(EXPERT) * so_far // total:
            order.append((EXPERT[done][0], b_experts, EXPERT[done][1]))
            done += 1
    return order


def of(batch, stages):
    return [(s, batch, k, weight) for s, k, weight in stages]


ORDER = beside(of(0, CROSS), None)
for b in range(NB):
    ORDER += beside((of(b - 1, REST) if b else []) + (of(b + 1, CROSS) if b + 1 < NB else []), b)
ORDER += beside(of(NB - 1, REST), None)
NORMS = [(b, {"cross_out": 1, "moe_out": 2, "linear_out": 3, "linear_norm": 4, "second_out": 5, "ffn_norm": 6}[s]) for s, b, k in ORDER
         if s in ("cross_out", "moe_out", "linear_out", "linear_norm", "second_out", "ffn_norm")]
NORM_NO = {x: n for n, x in enumerate(NORMS)}
WCOLS=4*P+NE+NE*F+2*NE*P+256+P+4*512+3*P

def build(nc, CN, RN, out, D):
    scr_t2 = nc.dram_tensor("scr_t2",(2,P,2*NP),BF16).ap()
    scr_v = nc.dram_tensor("scr_v",(2,P,P),F32).ap()
    with ExitStack() as ctx:
        sb=lambda n,s,t=F32: ctx.enter_context(nc.sbuf_tensor(n,s,t))
        def sem(n,per): return Sem(ctx.enter_context(nc.semaphore(n)),per)
        def sem2(n,per): return [sem(n+'0',per),sem(n+'1',per)]
        bank=[ctx.enter_context(nc.psum_tensor(f"bank{k}",[P,512],F32)) for k in range(8)]
        ps_proj=bank[0]
        ps_post=bank[1]
        ps_S=bank[2:4]
        ps_T=bank[4:6]
        ps_O=bank[6:8]
        ident=sb("ident",[P,P])
        ident_bf16=sb("ident_bf16",[P,P],BF16)
        x1=sb("x1",[P,NT,P])
        x1T=sb("x1T",[P,NT*P])
        probs=sb("probs",[P,2,H4,NP])
        mhalf=sb("mhalf",[P,4])
        x1_ve_done=sem("x1_ve_done",1)
        first_weights_in=sem("first_weights_in",0)
        consts=sem("consts",0)
        zeros=sem("zeros",0)
        xb_done=sem("xb_done",1)
        proj_ready=sem("proj_ready",1)
        xt_copied=sem("xt_copied",1)
        qkv_done=sem("qkv_done",1)
        first_part_done=sem("first_part_done",1)
        parts_done=sem("parts_done",4)
        parts_turned=sem("parts_turned",1)
        parts_out=sem2("parts_out",16)
        v_out=sem2("v_out",16)
        parts_in=sem2("parts_in",96)
        v_in=sem2("v_in",16)
        s_ready=sem("s_ready",11)
        s_max=sem("s_max",11)
        maxima_turned=sem("maxima_turned",1)
        maximaT_done=sem("maximaT_done",1)
        maxima_in=sem2("maxima_in",16)
        sT_ready=sem("sT_ready",11)
        exp_done=sem("exp_done",11)
        causal_done=sem("causal_done",4)
        pv_done=sem("pv_done",4)
        out_turned=sem("out_turned",1)
        recip_done=sem("recip_done",1)
        attn_done=sem("attn_done",1)
        attnT_ready=sem("attnT_ready",1)
        attnT_done=sem("attnT_done",1)
        out_ready=sem("out_ready",1)
        x1_sum_done=sem("x1_sum_done",1)
        x1_st_done=sem("x1_st_done",1)
        x1_stats_done=sem("x1_stats_done",1)
        x1_rstd_done=sem("x1_rstd_done",1)
        x1_ready=sem("x1_ready",1)
        x1T_ready=sem("x1T_ready",1)
        x1T_done=sem("x1T_done",1)
        x1_kept=sem("x1_kept",1)
        sems={}
        for k,v in PER_BATCH.items(): sems[k]=ctx.enter_context(nc.semaphore(k))
        def wait_batch(e,name,b,n):
            v=b*PER_BATCH[name]+n
            if v>0: e.wait_ge(sems[name],v)
        x_in=ctx.enter_context(nc.semaphore("x_in"))
        x0_in=ctx.enter_context(nc.semaphore("x0_in"))
        xt_in=ctx.enter_context(nc.semaphore("xt_in"))
        k_zeros=ctx.enter_context(nc.semaphore("k_zeros"))
        weights_in=ctx.enter_context(nc.semaphore("weights_in"))
        late_consts=ctx.enter_context(nc.semaphore("late_consts"))
        late_zeros=ctx.enter_context(nc.semaphore("late_zeros"))
        folded=ctx.enter_context(nc.semaphore("folded"))
        head_pick=sb("head_pick",[P,4,LG],BF16)
        head_pick_f=sb("head_pick_f",[P,4,4,L])
        ones_blocks=sb("ones_blocks",[P,3,4,DH])
        head_mask=sb("head_mask",[P,16,DH])
        names_w=dict(wq=P,wk=P,wv=P,wo=P,gate=NE,w1=NE*F,w2=NE*2*P,wkv1=256,wq1=P,Wq5=512,Wk5=512,Wv5=512,Wo5=512,Wr=P,Wk6=P,Wv6=P,cols=D['w_all'].shape[1]-WCOLS)
        W_CHUNK=D['w_all'].shape[1]//(NT-1)
        weights_all=sb("weights_all",[P,D['w_all'].shape[1]])
        weights={}
        o=0
        for n,k in names_w.items(): weights[n]=weights_all[:,o:o+k]; o+=k
        col=lambda n,j=0: weights['cols'][:,CN[n]+j:CN[n]+j+1]
        nrow=D['rows'].shape[1]
        rows=sb("rows",[P,nrow])
        row=lambda n,k: rows[:,RN[n]:RN[n]+k]
        b2=sb("b2",[NE,P])
        wo_gained=sb("wo_gained",[P,4,P])
        shift_out=sb("shift_out",[P,P])
        one_less_mu=sb("one_less_mu",[P,2])
        v_blocks=sb("v_blocks",[P,4,3,32])
        bounds=sb("bounds",[P,4,P],BF16)
        top2=sb("top2",[P,4,8])
        context_s=sb("context_s",[P,4,P])
        x5T=sb("x5T",[P,NQ+1])
        kv_s=sb("kv_s",[P,4,257])
        ctx_s=sb("ctx_s",[P,NB,L])
        v5_s=sb("v5_s",[L+1,512])
        with ExitStack() as first:
            sa=lambda n,s,t=F32: first.enter_context(nc.sbuf_tensor(n,s,t))
            maskT=sa("maskT",[P,P],BF16)
            maskf=sa("maskf",[P,P])
            wqkv_s=sa("wqkv_s",[P,384])
            wout_s=sa("wout_s",[P,P])
            bqkv_s=sa("bqkv_s",[P,384])
            bout_s=sa("bout_s",[P,P])
            x_bias=sa("x_bias",[P,NT,P])
            xT_s=sa("xT_s",[P,2,P])
            qkv=sa("qkv",[P,2,384])
            part_s=sa("part_s",[P,2,2,C,32],BF16)
            rest_s=sa("rest_s",[P,2,256])
            turned_parts=sa("turned_parts",[P,2,2,NP],BF16)
            q_parts=sa("q_parts",[P,4,H4,NP],BF16)
            k_parts=sa("k_parts",[P,4,H4,NP],BF16)
            v_ones=sa("v_ones",[P,4,16,32])
            maxima=sa("maxima",[P,2,16],BF16)
            maximaT=sa("maximaT",[16,P],BF16)
            out_heads=sa("out_heads",[P,C,32])
            recip_s=sa("recip_s",[P,C])
            attn=sa("attn",[P,C,DH])
            attnT=sa("attnT",[P,P])
            x1_sum=sa("x1_sum",[P,P])
            x1_st=sa("x1_st",[P,6])
            x1_mv=sa("x1_mv",[P,2])
            x1_rstd=sa("x1_rstd",[P,1])
            x1_ve=sa("x1_ve",[P,1])
            x1_tile=sa("x1_tile",[P,P])
        kT_s=sb("kT_s",[P,L])
        v_s=sb("v_s",[L,P])
        k_blocks=sb("k_blocks",[P,4,LG])
        k_bf16=sb("k_bf16",[P,16*L],BF16)
        q_s=sb("q_s",[P,NQ])
        q_bf16=sb("q_bf16",[P,NQ],BF16)
        boundsT=sb("boundsT",[P,NQ],BF16)
        denom_r=sb("denom_r",[P,NQ])
        heads=sb("heads",[P,NQ])
        x1b=sb("x1b",[P,4,P])
        norm_x=sb("norm_x",[P,4,P])
        norm_st=sb("norm_st",[P,4,6])
        norm_mv=sb("norm_mv",[P,4,2])
        norm_ve=sb("norm_ve",[P,4])
        norm_rstd=sb("norm_rstd",[P,4])
        x2=sb("x2",[P,2,4,P])
        x2T=sb("x2T",[P,2,NQ])
        logits=sb("logits",[P,4,NE])
        top8=sb("top8",[P,4,8])
        logits_rest=sb("logits_rest",[P,4,NE])
        chosen=sb("chosen",[P,4,NE])
        shifted=sb("shifted",[P,4,NE])
        gate_exp=sb("gate_exp",[P,4,NE])
        gates=sb("gates",[P,2,4,NE])
        gate_sum=sb("gate_sum",[P,4])
        gate_rec=sb("gate_rec",[P,4])
        gatesT=sb("gatesT",[NE,NQ])
        hidden=sb("hidden",[P,2,2,NQ])
        moe_sum=sb("moe_sum",[P,2,4,P])
        x3=sb("x3",[P,4,P])
        x3b=sb("x3b",[P,4,P])
        x3T=sb("x3T",[P,NQ])
        kv_sum=sb("kv_sum",[P,144])
        q1_s=sb("q1_s",[P,NQ])
        denoms=sb("denoms",[P,4,16])
        scratch=sb("scratch",[P,4,P])
        x4=sb("x4",[P,4,P])
        x4T=sb("x4T",[P,NQ])
        k5=sb("k5",[P,4,L+1])
        k5_neg_max=sb("k5_neg_max",[P,4])
        k5_e=sb("k5_e",[P,4,L+1])
        k5_sum=sb("k5_sum",[P,4])
        k5T=sb("k5T",[L+1,512])
        q5_st=sb("q5_st",[P,2,6])
        q5_mv=sb("q5_mv",[P,2,2])
        q5_ve=sb("q5_ve",[P,2])
        q5_rstd=sb("q5_rstd",[P,2])
        o5_st=sb("o5_st",[P,2,6])
        o5_mv=sb("o5_mv",[P,2,2])
        o5_ve=sb("o5_ve",[P,2])
        o5_rstd=sb("o5_rstd",[P,2])
        q5_n=sb("q5_n",[P,2,512])
        q5_z=sb("q5_z",[P,2,512])
        q5_max=sb("q5_max",[P,8])
        q5_e=sb("q5_e",[P,2,512])
        q5_sum=sb("q5_sum",[P,2,8])
        q5_eT=sb("q5_eT",[P,512])
        o5_s=sb("o5_s",[P,2,512])
        o5_n=sb("o5_n",[P,2,512])
        o5_nT=sb("o5_nT",[P,512])
        x5=sb("x5",[P,4,P])
        x6=sb("x6",[P,4,P])
        NW=NT-1+4
        block=ctx.enter_context(nc.Block())
        bc=lambda ap,shape: ap.broadcast_to(shape)
        mixed=q5_z
        xk=q5_n[:,0]
        xr=q5_n[:,1]
        k6_r=q5_e[:,0]
        k6_sq=q5_e[:,1]
        r6_s=q5_eT
        @block.sync
        def _(sp):
            for dst,src in ((wqkv_s[:],D['wqkv']),(wout_s[:],D['wout']),(bqkv_s[:],D['bqkv'].broadcast_to((P,384))),(bout_s[:],D['bout'].broadcast_to((P,P)))):
                sp.dma_start(dst,src).then_inc(first_weights_in.sem,16)
            sp.dma_start(x1T[:,0:P],D['xT'][:,0:P]).then_inc(x0_in,16)
            sp.dma_start(x1T[:,P:NT*P],D['xT'][:,P:NT*P]).then_inc(xt_in,16)
            small=((b2[:],D['b2']),(v5_s[L:L+1,:],D['nv']),(ctx_s[:],D['ctxT'].rearrange('b p l -> p b l')))
            broad=((rows[:],D['rows'].broadcast_to((P,nrow))),)
            def part(what, n, t):
                p=t.p
                wait_apart(sp,qkv_done,t,1)
                wait_dma_apart(sp,v_in,t-2)
                sp.dma_start(scr_v[p], qkv[:,p,256:384]).then_inc(v_out[p].sem,16)
                wait_apart(sp,parts_turned,t,1)
                wait_dma_apart(sp,parts_in,t-2)
                sp.dma_start(scr_t2[p], turned_parts[:,p].rearrange("p a n -> p (a n)")).then_inc(parts_out[p].sem,16)
                if t.first(1):
                    sp.dma_start(x_bias[:],D['x'].rearrange("(t p) f -> p t f",p=P)).then_inc(x_in,16)
                    sp.wait_ge(zeros.sem,4); sp.wait_ge(k_zeros,2)
                wait_dma_apart(sp,v_out,t)
                wait_apart(sp,pv_done,t-3)
                sp.dma_start(v_ones[:,t.q,:,0:DH], scr_v[p].rearrange("(g t) (c e) -> g (t c) e",t=8,e=DH).rearrange("g q e -> q g e")).then_inc(v_in[p].sem,16)
                wait_dma_apart(sp,parts_out,t)
                sd=scr_t2[p].rearrange("(r s) (a n) -> a s r n",r=H4,a=2)
                for dst,a,off,row in ((q_parts,0,0,0),(q_parts,0,0,24),(q_parts,0,8,48),(k_parts,1,0,0),(k_parts,1,8,24),(k_parts,1,0,48)):
                    sp.dma_start(dst[row:row+24,t.q], sd[a,off:off+24]).then_inc(parts_in[p].sem,16)
                for dst,src in {1:small,2:broad}.get(t.k if t.i is None else -1,()): sp.dma_start(dst,src).then_inc(weights_in,16)
                if not t.first(1):
                    sp.dma_start(weights_all[:,bass.ds((t.n-1)*W_CHUNK,W_CHUNK)],D['w_all'][:,bass.ds((t.n-1)*W_CHUNK,W_CHUNK)]).then_inc(weights_in,16)
            steps(sp,[("load",0,1)],part)
            sp.wait_ge(x1_kept.sem,NT)
            sp.wait_ge(x1T_done.sem,NT)
            def stage(s, b, k):
                if s == "keys":
                    wait_batch(sp,'v_done',b,1)
                    wait_batch(sp,'values_ready',b,0)
                    for hh,k0,k1,c,r0 in ((0,0,77,0,0),(1,0,51,0,77),(1,51,77,1,0),(2,0,77,1,26),(3,0,25,1,103),(3,25,77,2,0)):
                        sp.dma_start(v_blocks[r0:r0+k1-k0,:,c,hh*DH:hh*DH+DH],v_s[k0:k1,:].rearrange("k (g h e) -> k g h e",g=4,h=4)[:,:,hh]).then_inc(sems['v_blocks_in'],16)
                if s == "ffn_norm":
                    wait_batch(sp,'x6_done',b,4)
                    sp.dma_start(out[b:b+1].rearrange("o (t p) f -> p (o t) f",p=P),x6[:]).then_inc(sems['out_written'],16)
            for s,b,k in ORDER: stage(s,b,k)
            sp.wait_ge(sems['out_written'],16*NB)

        @block.gpsimd
        def _(g):
            n=[0]
            def c(ins):
                n[0]+=1
                ins.then_inc(consts.sem,1)
                g.wait_ge(consts.sem,n[0])
            c(g.memset(ident[:],0.0))
            c(g.affine_select(out=ident[:],in_=ident[:],compare_op=ALU.not_equal,fill=1.0,base=0,pattern=[[-1,P]],channel_multiplier=1))
            c(g.tensor_copy(ident_bf16[:],ident[:]))
            c(g.memset(maskf[:],0.0))
            c(g.affine_select(out=maskf[:],in_=maskf[:],compare_op=ALU.is_ge,fill=BIG,base=0,pattern=[[1,P]],channel_multiplier=-1))
            c(g.tensor_copy(maskT[:],maskf[:]))
            c(g.memset(mhalf[:],-0.5))
            g.memset(k_parts[64:128].rearrange("p q r n -> p (q r n)").bitcast(F32),0.0).then_inc(k_zeros,1)
            g.wait_ge(k_zeros,1)
            g.memset(k_parts[96:97],-1.0).then_inc(k_zeros,1)
            g.wait_ge(k_zeros,2)
            g.wait_ge(first_weights_in.sem,64)
            n=[0]
            def c(ins):
                n[0]+=1
                ins.then_inc(late_consts,1)
                g.wait_ge(late_consts,n[0])
            c(g.memset(head_mask[:],1.0))
            c(g.affine_select(out=head_mask[:],in_=head_mask[:],compare_op=ALU.is_ge,fill=0.0,base=0,pattern=[[-DH,16],[0,DH]],channel_multiplier=1))
            c(g.affine_select(out=head_mask[:],in_=head_mask[:],compare_op=ALU.is_ge,fill=0.0,base=DH-1,pattern=[[DH,16],[0,DH]],channel_multiplier=-1))
            c(g.memset(ones_blocks[:],1.0))
            c(g.affine_select(out=ones_blocks[:],in_=ones_blocks[:],compare_op=ALU.is_ge,fill=0.0,base=0,pattern=[[128,3],[-L,4],[0,DH]],channel_multiplier=1))
            c(g.affine_select(out=ones_blocks[:],in_=ones_blocks[:],compare_op=ALU.is_ge,fill=0.0,base=L-1,pattern=[[-128,3],[L,4],[0,DH]],channel_multiplier=-1))
            c(g.memset(head_pick_f[:],0.0))
            c(g.affine_select(out=head_pick_f[:],in_=head_pick_f[:],compare_op=ALU.not_equal,fill=-1.0,base=0,pattern=[[-4,4],[-1,4],[0,L]],channel_multiplier=1))
            c(g.tensor_copy(head_pick[:],head_pick_f[:].rearrange("p g h k -> p g (h k)")))
            def part(what, n, t):
                if what=="select":
                    wait_apart(g,exp_done,t,[4,8,10,11][n])
                    d=probs[:,n%2,:,0:P]
                    g.affine_select(out=d,in_=d,compare_op=ALU.is_ge,fill=0.0,base=0,pattern=[[0,H4],[1,P]],channel_multiplier=-1).then_inc(causal_done.sem,1)
                if what=="variance":
                    wait_apart(g,x1_stats_done,t,1)
                    g.tensor_scalar(x1_ve[:],x1_mv[:,1:2],1e-5,None,ALU.add).then_inc(x1_ve_done.sem,1)
                    wait(g,x1_ve_done,t,1)
                    g.tensor_tensor(x1_rstd[:],x1_ve[:],mhalf[:,0:1],ALU.pow).then_inc(x1_rstd_done.sem,1)
                if what=="x_bias":
                    d=x_bias[:,bass.ds(t.n,1),:].rearrange("p o f -> p (o f)")
                    if t.first(1): g.wait_ge(x_in,16)
                    g.tensor_tensor(d,d,bout_s[:],ALU.add).then_inc(xb_done.sem,1)
                if what=="keep":
                    wait(g,x1_ready,t,1)
                    g.tensor_copy(x1[:,bass.ds(t.n,1),:].rearrange("p o f -> p (o f)"),x1_tile[:]).then_inc(x1_kept.sem,1)
            steps(g,POOL_STEP,part)
            g.wait_ge(x1_kept.sem,NT)
            g.wait_ge(x1T_done.sem,NT)
            g.wait_ge(weights_in,16*NW)
            g.wait_ge(late_zeros,8)
            own=[0]
            def keep_on(ins):
                own[0]+=1
                ins.then_inc(sems['pool_own'],1)
            def settle(): g.wait_ge(sems['pool_own'],own[0])
            def norm_scale(b,k):
                n=NORM_NO[b,k]
                wait_batch(g,'norm_stats',n,1)
                wait_batch(g,'norm_scale',n,0)
                keep_on(g.tensor_scalar(norm_ve[:],norm_mv[:,:,1],1e-5,None,ALU.add))
                settle()
                g.tensor_tensor(norm_rstd[:],norm_ve[:],mhalf[:],ALU.pow).then_inc(sems['norm_scale'],1)
            def row_scale(b,t,stats,mvx,vv,r,done):
                p=t%2
                wait_batch(g,stats,b,t+1)
                wait_batch(g,done,b,t-1)
                keep_on(g.tensor_scalar(vv[:,p:p+1],mvx[:,p,1:2],1e-5,None,ALU.add))
                settle()
                g.tensor_tensor(r[:,p:p+1],vv[:,p:p+1],mhalf[:,0:1],ALU.pow).then_inc(sems[done],1)
            def stage(s, b, k):
                if s=="query":
                    if b: wait_batch(g,'norm_in',NORM_NO[b-1,1],1)
                    g.tensor_tensor(x1b[:],x1[:,4*b:4*b+4,:],bc(row('bo',P).unsqueeze(1),(P,4,P)),ALU.add).then_inc(sems['x1_bias_done'],1)
                if s=="cross_out": norm_scale(b,1)
                if s=="moe_out": norm_scale(b,2)
                if s=="linear":
                    wait_batch(g,'x3_done',b,4)
                    if b: wait_batch(g,'norm_in',NORM_NO[b-1,4],1)
                    g.tensor_tensor(x3b[:],x3[:],bc(row('beta',P).unsqueeze(1),(P,4,P)),ALU.add).then_inc(sems['x3_beta_done'],1)
                if s=="linear_out": norm_scale(b,3)
                if s=="linear_norm": norm_scale(b,4)
                if s=="second_out": norm_scale(b,5)
                if s=="ffn_norm": norm_scale(b,6)
                if s=="q": row_scale(b,k,'q5_stats',q5_mv,q5_ve,q5_rstd,'q5_scale')
                if s=="o": row_scale(b,k,'o5_stats',o5_mv,o5_ve,o5_rstd,'o5_scale')
            for s,b,k in ORDER: stage(s,b,k)

        @block.scalar
        def _(a):
            def part(what, n, t):
                p=t.p
                if what=="parts":
                    wait(a,qkv_done,t,1)
                    wait(a,parts_turned,t-1)
                    src=qkv[:,p,0:256].rearrange("p (m e) -> p m e",e=DH)
                    dst=part_s[:,p].rearrange("p a c (s e) -> p (a c) s e",e=DH)
                    a.activation(dst[:,:,0:4:3],src.unsqueeze(2).broadcast_to((P,32,2,DH)),ACT.Copy).then_inc(first_part_done.sem,1)
                if what=="x_copy":
                    if t.first(1): a.wait_ge(x0_in,16)
                    elif t.first(2): a.wait_ge(xt_in,16)
                    wait(a,proj_ready,t,-1)
                    a.activation(xT_s[:,t.p],x1T[:,bass.ds(t.n*P,P)],ACT.Copy).then_inc(xt_copied.sem,1)
                if what=="exp":
                    j,hs=UNITS_T[n]
                    k=len(hs)
                    N=P*(4-j)
                    wait(a,sT_ready,t,n+1)
                    wait(a,pv_done,t,j-1)
                    a.activation(probs[:,j%2,hs[0]:hs[0]+k,0:N], ps_T[(n+t.p)%2][:,0:k*N].rearrange("p (k n) -> p k n",k=k), ACT.Exp, scale=1/16.).then_inc(exp_done.sem,1)
                if what=="maxima":
                    wait(a,maxima_turned,t,1)
                    wait_dma(a,maxima_in,t-1)
                    a.activation(maximaT[:],ps_S[t.p][0:16,0:64].bitcast(BF16),ACT.Copy).then_inc(maximaT_done.sem,1)
                    wait(a,maximaT_done,t,1)
                    wait_dma(a,parts_in,t)
                    a.dma_start(q_parts[96:97,t.q].rearrange("o r (i n) -> o (r i) n",i=4),maximaT[:]).then_inc(maxima_in[t.p].sem,16)
                if what=="out_turn":
                    wait(a,attnT_ready,t,1)
                    a.activation(attnT[:],ps_post[:,0:P],ACT.Copy).then_inc(attnT_done.sem,1)
                if what=="x1_turn":
                    wait(a,x1T_ready,t,1)
                    a.activation(x1T[:,bass.ds(t.n*P,P)],ps_post[:,0:P],ACT.Copy).then_inc(x1T_done.sem,1)
            steps(a,ACT_STEP,part)
            a.wait_ge(x1_kept.sem,NT)
            a.wait_ge(x1T_done.sem,NT)
            def act(out_,in_,f,name,**k): a.activation(out_,in_,f,**k).then_inc(sems[name],1)
            def stage(s, b, k):
                p=b%2
                if s=="keys":
                    wait_batch(a,'kT_ready',b,1)
                    wait_batch(a,'k_bf16_done',b,0)
                    act(kT_s[:],bank[6][:,0:L],ACT.Identity,'kT_done',bias=col('bk'))
                if s=="query":
                    wait_batch(a,'q_ready',b,1)
                    wait_batch(a,'scores_ready',b,0)
                    act(q_s[:],bank[5][:],ACT.Identity,'q_done',bias=col('bq'))
                if s=="bound_turn":
                    wait_batch(a,'bound_turned',b,1)
                    act(boundsT[:].rearrange("p (t n) -> p t n",t=4),bank[7][:,0:256].bitcast(BF16).rearrange("p (t n) -> p t n",t=4),ACT.Copy,'boundT_done')
                if s=="scores":
                    for u in range(3*k,3*k+3):
                        c,gq=divmod(u,4)
                        w=CW[c]
                        wait_batch(a,'scores_ready',b,u+1)
                        wait_batch(a,'values_ready',b,c-1)
                        act(probs[0:w,c%2,gq],bank[T_BANKS[u%3]][0:w],ACT.Exp,'probs_done',scale=DH**-0.5)
                if s=="cross_turn":
                    wait_batch(a,'x2T_ready',b,1)
                    act(x2T[:,p],bank[3][:],ACT.Copy,'x2T_done')
                if s=="gate":
                    wait_batch(a,'logits_shifted',b,1)
                    act(gate_exp[:],shifted[:],ACT.Exp,'logits_exp')
                if s=="gate_turn":
                    wait_batch(a,'gates_turned',b,1)
                    act(gatesT[:],bank[7][0:NE,:],ACT.Copy,'gatesT_done')
                if s=="up":
                    for h in range(2):
                        u=2*k+h
                        wait_batch(a,'hidden_ready',b,u+1)
                        wait_batch(a,'expert_ready',b,k-1)
                        act(hidden[:,k%2,h],bank[h][:],ACT.Gelu,'hidden_done',bias=col('b1',u))
                if s=="moe_turn":
                    wait_batch(a,'x3T_ready',b,1)
                    act(x3T[:],bank[7][:],ACT.Copy,'x3T_done')
                if s=="linear":
                    wait_batch(a,'q1_ready',b,1)
                    act(q1_s[:],bank[5][:],ACT.Relu,'q1_done',bias=col('bq1'))
                if s=="context":
                    for j in range(4):
                        wait_batch(a,'k5_max_done',b,1)
                        wait_batch(a,'k5_turned',b,0)
                        a.activation(k5_e[:,j],k5[:,j],ACT.Exp,bias=k5_neg_max[:,j:j+1],accum_out=k5_sum[:,j:j+1]).then_inc(sems['k5_exp_done'],1)
                if s=="context_turn":
                    wait_batch(a,'k5_turned',b,1)
                    act(k5T[:],bank[7][0:L+1,:],ACT.Copy,'k5T_done')
                if s=="linear_turn":
                    wait_batch(a,'x4T_ready',b,1)
                    act(x4T[:],bank[3][:],ACT.Copy,'x4T_done')
                if s=="m":
                    wait_batch(a,'q5_less_max',b,k+1)
                    wait_batch(a,'q5_turned',b,k-1)
                    wait_batch(a,'q5_summed',b,k-1)
                    act(q5_e[:,k%2],q5_z[:,k%2],ACT.Exp,'q5_exp_done')
                if s=="a":
                    wait_batch(a,'q5_turned',b,k+1)
                    wait_batch(a,'o5_ready',b,k)
                    act(q5_eT[:],bank[7][:],ACT.Copy,'q5T_done')
                if s=="z":
                    wait_batch(a,'o5_turned',b,k+1)
                    wait_batch(a,'second_ready',b,k)
                    act(o5_nT[:],bank[6][:],ACT.Copy,'o5T_done')
                if s=="second_turn":
                    wait_batch(a,'x5T_ready',b,1)
                    wait_batch(a,'xk_done',b,0)
                    wait_batch(a,'xr_done',b,0)
                    act(x5T[:,1:NQ+1],bank[7][:],ACT.Copy,'x5T_done')
                if s=="ffn_in":
                    wait_batch(a,'k6_ready',b,1)
                    act(k6_r,bank[3][:],ACT.Relu,'k6_relu')
                    wait_batch(a,'k6_relu',b,1)
                    act(k6_sq,k6_r,ACT.Square,'k6_squared')
                    wait_batch(a,'r6_ready',b,1)
                    act(r6_s[:],bank[5][:],ACT.Sigmoid,'r6_sigmoid')
            a.wait_ge(weights_in,16*NW)
            a.wait_ge(late_consts,9)
            for s,b,k in ORDER: stage(s,b,k)

        @block.vector
        def _(v):
            n=[0]
            def c(ins):
                n[0]+=1
                ins.then_inc(zeros.sem,1)
                v.wait_ge(zeros.sem,n[0])
            flat=lambda z: z.rearrange("p q r n -> p (q r n)").bitcast(F32)
            nz=[0]
            def c2(ins):
                nz[0]+=1
                ins.then_inc(late_zeros,1)
                v.wait_ge(late_zeros,nz[0])
            c(v.memset(part_s[:],0.0))
            def zeros_and_ones():
                c(v.memset(flat(q_parts[64:128]),0.0))
                c(v.memset(v_ones[:],0.0))
                c(v.memset(v_ones[:,:,:,DH:DH+1],1.0))
                c2(v.memset(v_blocks[:],0.0))
                c2(v.memset(bounds[:],0.0))
                c2(v.memset(top2[:],3e38))
                c2(v.memset(context_s[:],0.0))
                c2(v.memset(x5T[:,0:1],0.0))
                c2(v.memset(kv_s[:,:,128:129],1.0))
            def part(what, n, t):
                p=t.p
                dst=part_s[:,p].rearrange("p a c (s e) -> p (a c) s e",e=DH)
                r1=rest_s[:,p].rearrange("p (m e) -> p m e",e=DH)
                if what=="bias":
                    wait(v,proj_ready,t,1)
                    wait_dma(v,v_out,t-2)
                    wait(v,parts_done,t-1)
                    v.tensor_tensor(qkv[:,p,:],ps_proj[:,0:384],bqkv_s[:],ALU.add).then_inc(qkv_done.sem,1)
                if what=="parts" and n==1:
                    wait(v,qkv_done,t,1)
                    wait(v,first_part_done,t,1)
                    v.tensor_tensor(r1,qkv[:,p,0:256].rearrange("p (m e) -> p m e",e=DH),dst[:,:,0],ALU.subtract).then_inc(parts_done.sem,1)
                if what=="parts" and n==2:
                    wait(v,parts_done,t,1)
                    v.tensor_copy(dst[:,:,1],r1).then_inc(parts_done.sem,1)
                if what=="parts" and n==3:
                    wait(v,parts_done,t,2)
                    v.tensor_tensor(dst[:,:,2],r1,dst[:,:,1],ALU.subtract).then_inc(parts_done.sem,1)
                if what=="heads":
                    if n==0: wait(v,parts_done,t,3); wait_dma(v,parts_out,t-2)
                    v.transpose(turned_parts[:,p,n].rearrange("p (t c) -> p c t",c=C),part_s[:,p,n]).then_inc((parts_done,parts_turned)[n].sem,1)
                    if n==1 and t.first(1): zeros_and_ones()
                if what=="max":
                    i,hs=UNITS_S[n]
                    k=len(hs)
                    N=P*(i+1)
                    wait(v,s_ready,t,n+1)
                    if n==0: wait(v,maxima_turned,t-1)
                    v.tensor_reduce(maxima[:,p].rearrange("p (r i) -> p r i",i=4)[:,hs[0]:hs[0]+k,i],ps_S[(n+t.p)%2][:,0:k*N].rearrange("p (k n) -> p k n",k=k),AX.X,ALU.max).then_inc(s_max.sem,1)
                if what=="out_turn":
                    wait(v,pv_done,t,4)
                    wait(v,attn_done,t)
                    v.transpose(out_heads[:], ps_O[p][:].rearrange("p (t c) -> p c t",c=C)).then_inc(out_turned.sem,1)
                if what=="norm":
                    wait(v,out_turned,t,1)
                    v.reciprocal(recip_s[:],out_heads[:,:,DH]).then_inc(recip_done.sem,1)
                    wait(v,recip_done,t,1)
                    wait(v,attnT_ready,t)
                    v.tensor_tensor(attn[:],out_heads[:,:,0:DH],recip_s[:].unsqueeze(2).broadcast_to((P,C,DH)),ALU.mult).then_inc(attn_done.sem,1)
                if what=="sum":
                    wait(v,out_ready,t,1)
                    wait(v,xb_done,t,1)
                    v.tensor_tensor(x1_sum[:],ps_post[:,P:2*P],x_bias[:,bass.ds(t.n,1),:].rearrange("p o f -> p (o f)"),ALU.add).then_inc(x1_sum_done.sem,1)
                    wait(v,x1_sum_done,t,1)
                    v.bn_stats(x1_st[:],x1_sum[:]).then_inc(x1_st_done.sem,1)
                    wait(v,x1_rstd_done,t)
                    wait_apart(v,x1_st_done,t,1)
                    v.bn_aggr(x1_mv[:],x1_st[:]).then_inc(x1_stats_done.sem,1)
                if what=="x1":
                    wait(v,x1_rstd_done,t,1)
                    wait(v,x1T_ready,t)
                    wait(v,x1_kept,t)
                    v.tensor_scalar(x1_tile[:],x1_sum[:],x1_mv[:,0:1],x1_rstd[:],ALU.subtract,ALU.mult).then_inc(x1_ready.sem,1)
            steps(v,DVE_STEP,part)
            v.wait_ge(x1_kept.sem,NT)
            v.wait_ge(x1T_done.sem,NT)
            v.wait_ge(late_consts,9)
            v.wait_ge(weights_in,16*NW)
            c2(v.tensor_scalar(one_less_mu[:],weights['cols'][:,CN['mu']:CN['mu']+2],-1.0,1.0,ALU.mult,ALU.add))
            c2(v.tensor_copy(k5[:,:,L:L+1],bc(col('nk').unsqueeze(1),(P,4,1))))
            for j in range(4): v.tensor_scalar(wo_gained[:,j],weights['Wo5'][:,j*P:j*P+P],col('lng',j),None,ALU.mult).then_inc(folded,1)
            v.wait_ge(folded,5)
            v.tensor_copy(shift_out[:],bank[0][:,0:P]).then_inc(folded,1)
            v.wait_ge(folded,6)
            chain=[0]
            def do(ins):
                chain[0]+=1
                ins.then_inc(sems['dve_own'],1)
            def settle(): v.wait_ge(sems['dve_own'],chain[0])
            def signal(ins,name): ins.then_inc(sems[name],1)
            def stats(b,k):
                n=NORM_NO[b,k]
                wait_batch(v,'norm_in',n,1)
                for t in range(4): do(v.bn_stats(norm_st[:,t],norm_x[:,t]))
                wait_batch(v,'norm_scale',n,0)
                settle()
                for t in range(4):
                    i=v.bn_aggr(norm_mv[:,t],norm_st[:,t])
                    if t<3: do(i)
                    else: signal(i,'norm_stats')
            def norm(b,k,dst,name):
                n=NORM_NO[b,k]
                wait_batch(v,'norm_scale',n,1)
                wait_batch(v,'norm_stats',n,1)
                settle()
                for t in range(4):
                    signal(v.tensor_scalar(dst[:,t],norm_x[:,t],norm_mv[:,t,0:1],norm_rstd[:,t:t+1],ALU.subtract,ALU.mult),name)
            def experts_add(b,e):
                p=b%2
                wait_batch(v,'expert_ready',b,e+1)
                wait_batch(v,'moe_begun',b,1)
                wait_batch(v,'expert_added',b,4*e)
                for t in range(4):
                    signal(v.scalar_tensor_tensor(out=moe_sum[:,p,t],in0=bank[2][:,t*P:t*P+P],scalar=gates[:,p,t,e:e+1],in1=moe_sum[:,p,t],op0=ALU.mult,op1=ALU.add),'expert_added')
            def stage(s, b, k):
                p=b%2
                if s=="keys":
                    wait_batch(v,'v_ready',b,1)
                    wait_batch(v,'v_blocks_in',b,0)
                    signal(v.tensor_tensor(v_s[:],bank[7][0:L,0:P],row('bv',P)[0:L],ALU.add),'v_done')
                    wait_batch(v,'kT_done',b,1)
                    wait_batch(v,'scores_ready',b,0)
                    hk=lambda z: z.rearrange("p (h k) -> p h k",k=L)
                    signal(v.tensor_tensor(hk(k_blocks[:].rearrange("p g k -> p (g k)")),bc(kT_s[:].unsqueeze(1),(P,16,L)),bc(head_mask[:,:,0:1],(P,16,L)),ALU.mult),'k_spread')
                    wait_batch(v,'k_spread',b,1)
                    signal(v.tensor_copy(k_bf16[:],k_blocks[:].rearrange("p g k -> p (g k)")),'k_bf16_done')
                if s=="query":
                    wait_batch(v,'q_ready',b,1)
                    wait_batch(v,'q_done',b,1)
                    signal(v.tensor_scalar(q_bf16[:],bank[5][:],col('bq'),None,ALU.add),'q_bf16_done')
                if s=="bound":
                    for j,(h0,h1) in enumerate(((0,6),(6,12),(12,16))):
                        wait_batch(v,'bound_ready',b,3*k+j+1)
                        signal(v.tensor_reduce(bounds[:,k,h0:h1],bank[S_BANKS[j]][:,0:(h1-h0)*L].rearrange("p (h k) -> p h k",k=L),AX.X,ALU.max),'bound_done')
                if s=="cross_out":
                    for h in range(2):
                        c=slice(256*h,256*h+256)
                        wait_batch(v,'values_ready',b,3)
                        do(v.reciprocal(denom_r[:,c],bank[6][:,c]))
                        settle()
                        signal(v.tensor_tensor(heads[:,c],bank[5][:,c],denom_r[:,c],ALU.mult),'heads_done')
                    wait_batch(v,'cross_ready',b,1)
                    wait_batch(v,'x1_bias_done',b,1)
                    signal(v.tensor_tensor(norm_x[:],bank[7][:].rearrange("p (t f) -> p t f",t=4),x1b[:],ALU.add),'norm_in')
                    stats(b,1)
                    norm(b,1,x2[:,p],'x2_done')
                if s=="gate":
                    wait_batch(v,'logits_ready',b,1)
                    do(v.tensor_copy(logits[:],bank[4][:,0:64].rearrange("p (t e) -> p t e",t=4)[:,:,0:NE]))
                    settle()
                    for t in range(4): do(v.max(top8[:,t],logits[:,t]))
                    settle()
                    do(v.tensor_copy(top2[:,:,0:2],top8[:,:,0:2]))
                    signal(v.tensor_tensor(shifted[:],logits[:],bc(top8[:,:,0:1],(P,4,NE)),ALU.subtract),'logits_shifted')
                    settle()
                    for t in range(4): do(v.match_replace(logits_rest[:,t],top2[:,t],logits[:,t],-3e38))
                    settle()
                    do(v.tensor_tensor(chosen[:],logits[:],logits_rest[:],ALU.not_equal))
                    settle()
                    wait_batch(v,'logits_exp',b,1)
                    do(v.tensor_tensor(gates[:,p],gate_exp[:],chosen[:],ALU.mult))
                    settle()
                    do(v.tensor_reduce(gate_sum[:],gates[:,p],AX.X,ALU.add))
                    settle()
                    do(v.reciprocal(gate_rec[:],gate_sum[:]))
                    settle()
                    signal(v.tensor_tensor(gates[:,p],gates[:,p],bc(gate_rec[:].unsqueeze(2),(P,4,NE)),ALU.mult),'gates_done')
                if s=="gate_bias":
                    wait_batch(v,'gate_bias_ready',b,1)
                    wait_batch(v,'x2_done',b,4)
                    signal(v.tensor_tensor(moe_sum[:,p],bank[3][:].rearrange("p (t f) -> p t f",t=4),x2[:,p],ALU.add),'moe_begun')
                if s=="down": experts_add(b,k)
                if s=="moe_out":
                    wait_batch(v,'expert_added',b,4*NE)
                    do(v.tensor_scalar(moe_sum[:,p],moe_sum[:,p],-100.0,100.0,ALU.max,ALU.min))
                    settle()
                    signal(v.tensor_tensor(norm_x[:],moe_sum[:,p],x2[:,p],ALU.add),'norm_in')
                    stats(b,2)
                    norm(b,2,x3,'x3_done')
                if s=="linear":
                    for h in range(2):
                        wait_batch(v,'kv_ready',b,h+1)
                        r=row('bkv1',256)
                        src=bank[3+h][:].rearrange("p (t f) -> p t f",t=2)
                        do(v.tensor_tensor(kv_s[:,2*h:2*h+2,0:128],src[:,:,128:256],bc(r[:,128:256].unsqueeze(1),(P,2,P)),ALU.add))
                        do(v.tensor_tensor(kv_s[:,2*h:2*h+2,129:257],src[:,:,0:128],bc(r[:,0:128].unsqueeze(1),(P,2,P)),ALU.add))
                        settle()
                        signal(v.tensor_scalar(kv_s[:,2*h:2*h+2,129:257],kv_s[:,2*h:2*h+2,129:257],0.0,None,ALU.max),'kv_done')
                if s=="linear_sum":
                    wait_batch(v,'kv_sum_ready',b,1)
                    signal(v.tensor_tensor(kv_sum[:,0:128],bank[6][:,0:128],head_mask[:].rearrange("p h e -> p (h e)"),ALU.mult),'kv_sum_done')
                    signal(v.tensor_scalar(kv_sum[:,128:144],head_mask[:,:,0],bank[6][:,128:129],None,ALU.mult),'kv_sum_done')
                if s=="linear_out":
                    for h in range(2):
                        wait_batch(v,'linear_ready',b,h+1)
                        src=bank[3+h][:,0:288].rearrange("p (t f) -> p t f",t=2)
                        do(v.tensor_scalar(denoms[:,2*h:2*h+2],src[:,:,128:144],1e-6,None,ALU.max))
                        settle()
                        do(v.reciprocal(denoms[:,2*h:2*h+2],denoms[:,2*h:2*h+2]))
                        settle()
                        for t in range(2):
                            do(v.tensor_tensor(scratch[:,2*h+t].rearrange("p (h e) -> p h e",e=DH),src[:,t,0:128].rearrange("p (h e) -> p h e",e=DH),bc(denoms[:,2*h+t].unsqueeze(2),(P,16,DH)),ALU.mult))
                    settle()
                    wait_batch(v,'x3_done',b,4)
                    signal(v.tensor_tensor(norm_x[:],scratch[:],x3[:],ALU.add),'norm_in')
                    stats(b,3)
                    wait_batch(v,'norm_stats',NORM_NO[b,3],1)
                    settle()
                    for t in range(4): do(v.scalar_tensor_tensor(out=scratch[:,t],in0=norm_x[:,t],scalar=norm_mv[:,t,0:1],in1=row('gamma',P),op0=ALU.subtract,op1=ALU.mult))
                if s=="linear_norm":
                    wait_batch(v,'norm_scale',NORM_NO[b,3],1)
                    wait_batch(v,'x3_beta_done',b,1)
                    settle()
                    for t in range(4):
                        i=v.scalar_tensor_tensor(out=norm_x[:,t],in0=scratch[:,t],scalar=norm_rstd[:,t:t+1],in1=x3b[:,t],op0=ALU.mult,op1=ALU.add)
                        if t<3: do(i)
                        else: signal(i,'norm_in')
                    stats(b,4)
                    norm(b,4,x4,'x4_done')
                if s=="context":
                    wait_batch(v,'k5_ready',b,1)
                    wait_batch(v,'k5_exp_done',b,0)
                    do(v.tensor_copy(k5[:,:,0:L],bank[5][:,0:4*L].rearrange("p (j l) -> p j l",j=4)))
                    settle()
                    do(v.tensor_reduce(k5_neg_max[:],k5[:],AX.X,ALU.max))
                    settle()
                    signal(v.tensor_scalar(k5_neg_max[:],k5_neg_max[:],-1.0,None,ALU.mult),'k5_max_done')
                    wait_batch(v,'v5_ready',b,1)
                    wait_batch(v,'context_ready',b,0)
                    signal(v.tensor_copy(v5_s[0:L,:],bank[6][0:L,:]),'v5_done')
                if s=="context_turn":
                    wait_batch(v,'k5_exp_done',b,4)
                    do(v.reciprocal(k5_sum[:],k5_sum[:]))
                    settle()
                    for j in range(4): signal(v.tensor_scalar(k5_e[:,j],k5_e[:,j],k5_sum[:,j:j+1],8.0,ALU.mult,ALU.mult),'k5_normed')
                if s=="context_out":
                    wait_batch(v,'context_ready',b,1)
                    wait_batch(v,'o5_ready',b,0)
                    for h in range(2):
                        c=slice(64*h,64*h+64)
                        signal(v.tensor_copy(context_s[c,:,64*h:64*h+64],bank[5][c,:].rearrange("p (j e) -> p j e",j=4)[:,:,64*h:64*h+64]),'context_done')
                if s=="q":
                    wait_batch(v,'q5_ready',b,k+1)
                    wait_batch(v,'q5_scale',b,k-1)
                    do(v.bn_stats(q5_st[:,k%2],bank[3][:]))
                    settle()
                    signal(v.bn_aggr(q5_mv[:,k%2],q5_st[:,k%2]),'q5_stats')
                    wait_batch(v,'q5_stats',b,k+1)
                    signal(v.scalar_tensor_tensor(out=q5_n[:,k%2],in0=bank[3][:],scalar=q5_mv[:,k%2,0:1],in1=row('ln_q_g',512),op0=ALU.subtract,op1=ALU.mult),'q5_normed')
                if s=="m":
                    wait_batch(v,'q5_scale',b,k+1)
                    wait_batch(v,'q5_normed',b,k+1)
                    wait_batch(v,'q5_exp_done',b,k-1)
                    do(v.scalar_tensor_tensor(out=q5_z[:,k%2],in0=q5_n[:,k%2],scalar=q5_rstd[:,k%2:k%2+1],in1=row('ln_q_b',512),op0=ALU.mult,op1=ALU.add))
                    settle()
                    zz=q5_z[:,k%2].rearrange("p (h d) -> p h d",h=8)
                    do(v.tensor_reduce(q5_max[:],zz,AX.X,ALU.max))
                    settle()
                    signal(v.tensor_tensor(zz,zz,bc(q5_max[:].unsqueeze(2),(P,8,64)),ALU.subtract),'q5_less_max')
                if s=="a":
                    wait_batch(v,'q5_exp_done',b,k+1)
                    signal(v.tensor_reduce(q5_sum[:,k%2],q5_e[:,k%2].rearrange("p (h d) -> p h d",h=8),AX.X,ALU.add),'q5_summed')
                    wait_batch(v,'q5_summed',b,k+1)
                    do(v.reciprocal(q5_sum[:,k%2],q5_sum[:,k%2]))
                if s=="o":
                    wait_batch(v,'o5_ready',b,k+1)
                    wait_batch(v,'o5_normed',b,k-1)
                    settle()
                    signal(v.tensor_tensor(o5_s[:,k%2].rearrange("p (h d) -> p h d",h=8),bank[5][:].rearrange("p (h d) -> p h d",h=8),bc(q5_sum[:,k%2].unsqueeze(2),(P,8,64)),ALU.mult),'o5_done')
                    wait_batch(v,'o5_done',b,k+1)
                    do(v.bn_stats(o5_st[:,k%2],o5_s[:,k%2]))
                    wait_batch(v,'o5_scale',b,k-1)
                    settle()
                    signal(v.bn_aggr(o5_mv[:,k%2],o5_st[:,k%2]),'o5_stats')
                if s=="z":
                    wait_batch(v,'o5_scale',b,k+1)
                    wait_batch(v,'o5_stats',b,k+1)
                    wait_batch(v,'o5_turned',b,k-1)
                    signal(v.tensor_scalar(o5_n[:,k%2],o5_s[:,k%2],o5_mv[:,k%2,0:1],o5_rstd[:,k%2:k%2+1],ALU.subtract,ALU.mult),'o5_normed')
                if s=="second_out":
                    wait_batch(v,'x4_done',b,4)
                    do(v.tensor_tensor(scratch[:],x4[:],bc(shift_out[:].unsqueeze(1),(P,4,P)),ALU.add))
                    settle()
                    wait_batch(v,'second_ready',b,4)
                    signal(v.tensor_tensor(norm_x[:],bank[4][:].rearrange("p (t f) -> p t f",t=4),scratch[:],ALU.add),'norm_in')
                    stats(b,5)
                    norm(b,5,x5,'x5_done')
                if s=="second_turn":
                    wait_batch(v,'x5T_done',b,1)
                    signal(v.tensor_scalar(mixed[:,1],x5T[:,1:NQ+1],col('mu',1),None,ALU.mult),'x5_mixed')
                    wait_batch(v,'x5_mixed',b,1)
                    wait_batch(v,'k6_ready',b,0)
                    signal(v.scalar_tensor_tensor(out=xk,in0=x5T[:,0:NQ],scalar=one_less_mu[:,1:2],in1=mixed[:,1],op0=ALU.mult,op1=ALU.add),'xk_done')
                    signal(v.tensor_scalar(mixed[:,0],x5T[:,1:NQ+1],col('mu',0),None,ALU.mult),'x5_mixed')
                    wait_batch(v,'x5_mixed',b,2)
                    wait_batch(v,'r6_ready',b,0)
                    signal(v.scalar_tensor_tensor(out=xr,in0=x5T[:,0:NQ],scalar=one_less_mu[:,0:1],in1=mixed[:,0],op0=ALU.mult,op1=ALU.add),'xr_done')
                if s=="ffn_out":
                    wait_batch(v,'r6_sigmoid',b,1)
                    wait_batch(v,'v6_ready',b,1)
                    signal(v.tensor_tensor(scratch[:].rearrange("p t f -> p (t f)"),bank[6][:],r6_s[:],ALU.mult),'gated_done')
                if s=="ffn_norm":
                    wait_batch(v,'x5_done',b,4)
                    wait_batch(v,'gated_done',b,1)
                    signal(v.tensor_tensor(norm_x[:],scratch[:],x5[:],ALU.add),'norm_in')
                    stats(b,6)
                    wait_batch(v,'out_written',b,0)
                    norm(b,6,x6,'x6_done')
            for s,b,k in ORDER: stage(s,b,k)

        @block.tensor
        def _(pe):
            pe.wait_ge(first_weights_in.sem,64)
            def part(what, n, t):
                if what=="project":
                    wait(pe,xt_copied,t,1)
                    wait(pe,qkv_done,t)
                    pe.matmul(ps_proj[:,0:384],xT_s[:,t.p],wqkv_s[:],start=True,stop=True).then_inc(proj_ready.sem,1)
                if what=="S":
                    i,hs=UNITS_S[n]
                    N=P*(i+1)
                    if n==0 and t.first(1): pe.wait_ge(consts.sem,7)
                    if n==0: wait_dma(pe,parts_in,t); wait_dma(pe,v_in,t)
                    wait(pe,s_max,t,n-1)
                    if n==1: wait(pe,maximaT_done,t)
                    for k,r in enumerate(hs):
                        pe.matmul(ps_S[(n+t.p)%2][:,k*N:(k+1)*N],q_parts[0:96,t.q,r,P*i:P*i+P],k_parts[0:96,t.q,r,0:N],start=True,stop=False)
                        l=pe.matmul(ps_S[(n+t.p)%2][:,k*N+P*i:(k+1)*N],maskT[:],ident_bf16[:],start=False,stop=True)
                    l.then_inc(s_ready.sem,1)
                if what=="maxima":
                    wait(pe,s_max,t,11)
                    pe.transpose(ps_S[t.p][0:16,0:64].bitcast(BF16),maxima[:,t.p],ident_bf16[:]).then_inc(maxima_turned.sem,1)
                if what=="T":
                    j,hs=UNITS_T[n]
                    N=P*(4-j)
                    if n==0: wait_dma(pe,maxima_in,t)
                    wait(pe,exp_done,t,n-1)
                    for k,r in enumerate(hs):
                        l=pe.matmul(ps_T[(n+t.p)%2][:,k*N:(k+1)*N],k_parts[0:97,t.q,r,P*j:P*j+P],q_parts[0:97,t.q,r,P*j:NP],start=True,stop=True)
                    l.then_inc(sT_ready.sem,1)
                if what=="PV":
                    N=P*(4-n)
                    wait(pe,causal_done,t,n+1)
                    if n==0: wait(pe,out_turned,t-1)
                    for r in range(H4):
                        l=pe.matmul(ps_O[t.p][32*r:32*r+32,P*n:NP],v_ones[:,t.q,4*r+n,:],probs[:,n%2,r,0:N],start=(n==0),stop=(n==3))
                    l.then_inc(pv_done.sem,1)
                if what=="out_turn":
                    wait(pe,attn_done,t,1)
                    wait(pe,x1T_done,t)
                    pe.transpose(ps_post[:,0:P],attn[:].rearrange("p c e -> p (c e)"),ident[:]).then_inc(attnT_ready.sem,1)
                if what=="out":
                    wait(pe,attnT_done,t,1)
                    pe.matmul(ps_post[:,P:2*P],attnT[:],wout_s[:],start=True,stop=True).then_inc(out_ready.sem,1)
                if what=="x1_turn":
                    wait(pe,x1_ready,t,1)
                    pe.transpose(ps_post[:,0:P],x1_tile[:],ident[:]).then_inc(x1T_ready.sem,1)
            steps(pe,PE_STEP,part)
            pe.wait_ge(x1_kept.sem,NT)
            pe.wait_ge(x1T_done.sem,NT)
            pe.wait_ge(weights_in,16*NW)
            pe.wait_ge(late_consts,9)
            pe.wait_ge(late_zeros,8)
            pe.wait_ge(folded,4)
            for j in range(4): l=pe.matmul(bank[0][:,0:P],bc(col('lnb',j),(P,P)),weights['Wo5'][:,j*P:j*P+P],start=j==0,stop=j==3)
            l.then_inc(folded,1)
            pe.wait_ge(folded,6)
            mm=lambda o,l,r,s=True,e=True: pe.matmul(o,l,r,start=s,stop=e)
            def signal(ins,name): ins.then_inc(sems[name],1)
            def turn(src,b,name,bank_,pn,count=4):
                for t in range(4):
                    wait_batch(pe,name,b,t+1)
                    l=pe.transpose(bank_[:,t*P:t*P+P],src[:,t],ident[:])
                signal(l,pn)
            def stage(s, b, k):
                p=b%2
                ctx_b=ctx_s[:,b]
                if s=="keys":
                    wait_batch(pe,'gated_done',b-1,0)
                    signal(mm(bank[6][:,0:L],weights['wk'][:],ctx_b),'kT_ready')
                    signal(mm(bank[7][0:L,0:P],ctx_b,weights['wv'][:]),'v_ready')
                if s=="query":
                    wait_batch(pe,'gated_done',b-1,0)
                    signal(mm(bank[5][:],weights['wq'][:],x1T[:,b*NQ:b*NQ+NQ]),'q_ready')
                if s=="bound":
                    if k==0: wait_batch(pe,'k_bf16_done',b,1); wait_batch(pe,'q_bf16_done',b,1)
                    for j,(h0,h1) in enumerate(((0,6),(6,12),(12,16))):
                        if k: wait_batch(pe,'bound_done',b,3*(k-1)+j+1)
                        signal(mm(bank[S_BANKS[j]][:,0:(h1-h0)*L],q_bf16[:,k*P:k*P+P],k_bf16[:,h0*L:h1*L]),'bound_ready')
                if s=="bound_turn":
                    wait_batch(pe,'bound_done',b,12)
                    wait_batch(pe,'v_done',b,1)
                    m7=bank[7][:,0:256].bitcast(BF16)
                    for t in range(4): l=pe.transpose(m7[:,t*P:t*P+P],bounds[:,t],ident_bf16[:])
                    signal(l,'bound_turned')
                if s=="scores":
                    if k==0: wait_batch(pe,'boundT_done',b,1); wait_batch(pe,'q_done',b,1); wait_batch(pe,'k_spread',b,1)
                    for u in range(3*k,3*k+3):
                        c,gq=divmod(u,4)
                        w=CW[c]
                        if u>=3: wait_batch(pe,'probs_done',b,u-2)
                        r=slice(c*128,c*128+w)
                        mm(bank[T_BANKS[u%3]][0:w],k_blocks[:,gq,r],q_s[:],True,False)
                        signal(mm(bank[T_BANKS[u%3]][0:w],head_pick[:,gq,r],boundsT[:],False,True),'scores_ready')
                if s=="values":
                    c=k
                    w=CW[c]
                    wait_batch(pe,'probs_done',b,4*c+4)
                    if c==0: wait_batch(pe,'v_blocks_in',b,96)
                    for gq in range(4): mm(bank[5][32*gq:32*gq+32],v_blocks[0:w,gq,c],probs[0:w,c%2,gq],c==0,c==2)
                    for gq in range(4): l=mm(bank[6][32*gq:32*gq+32],ones_blocks[0:w,c].rearrange("p h e -> p (h e)"),probs[0:w,c%2,gq],c==0,c==2)
                    signal(l,'values_ready')
                if s=="cross_out":
                    for t in range(4):
                        wait_batch(pe,'heads_done',b,t//2+1)
                        l=mm(bank[7][:,t*P:t*P+P],heads[:,t*P:t*P+P],weights['wo'][:])
                    signal(l,'cross_ready')
                if s=="cross_turn": turn(x2[:,p],b,'x2_done',bank[3],'x2T_ready')
                if s=="gate":
                    wait_batch(pe,'x2T_done',b,1)
                    for t in range(4): l=mm(bank[4][:,t*16:t*16+NE],x2T[:,p,t*P:t*P+P],weights['gate'][:])
                    signal(l,'logits_ready')
                if s=="gate_turn":
                    wait_batch(pe,'gates_done',b,1)
                    for t in range(4): l=pe.transpose(bank[7][0:NE,t*P:t*P+P],gates[:,p,t],ident[:])
                    signal(l,'gates_turned')
                if s=="gate_bias":
                    wait_batch(pe,'gatesT_done',b,1)
                    for t in range(4): l=mm(bank[3][:,t*P:t*P+P],gatesT[:,t*P:t*P+P],b2[:])
                    signal(l,'gate_bias_ready')
                if s=="up":
                    wait_batch(pe,'x2T_done',b,1)
                    for h in range(2):
                        wait_batch(pe,'hidden_done',b,2*k+h-1)
                        signal(mm(bank[h][:],weights['w1'][:,k*F+h*P:k*F+h*P+P],x2T[:,p]),'hidden_ready')
                if s=="down":
                    wait_batch(pe,'hidden_done',b,2*k+2)
                    wait_batch(pe,'expert_added',b,4*k)
                    for t in range(4):
                        for h in range(2):
                            l=mm(bank[2][:,t*P:t*P+P],hidden[:,k%2,h,t*P:t*P+P],weights['w2'][:,(2*k+h)*P:(2*k+h+1)*P],h==0,h==1)
                    signal(l,'expert_ready')
                if s=="moe_turn": turn(x3,b,'x3_done',bank[7],'x3T_ready')
                if s=="linear":
                    wait_batch(pe,'x3T_done',b,1)
                    for t in range(4):
                        l=mm(bank[3+t//2][:,(t%2)*256:(t%2)*256+256],x3T[:,t*P:t*P+P],weights['wkv1'][:])
                        if t%2: signal(l,'kv_ready')
                    signal(mm(bank[5][:],weights['wq1'][:],x3T[:]),'q1_ready')
                if s=="linear_sum":
                    wait_batch(pe,'kv_done',b,2)
                    for t in range(4): l=mm(bank[6][:,0:129],kv_s[:,t,129:257],kv_s[:,t,0:129],t==0,t==3)
                    signal(l,'kv_sum_ready')
                if s=="linear_out":
                    wait_batch(pe,'kv_sum_done',b,2)
                    wait_batch(pe,'q1_done',b,1)
                    for t in range(4):
                        l=mm(bank[3+t//2][:,(t%2)*144:(t%2)*144+144],q1_s[:,t*P:t*P+P],kv_sum[:])
                        if t%2: signal(l,'linear_ready')
                if s=="context":
                    for j in range(4): l=mm(bank[5][:,j*L:(j+1)*L],weights['Wk5'][:,j*P:j*P+P],ctx_b)
                    signal(l,'k5_ready')
                    signal(mm(bank[6][0:L,:],ctx_b,weights['Wv5'][:]),'v5_ready')
                if s=="context_turn":
                    wait_batch(pe,'k5_normed',b,4)
                    for j in range(4): l=pe.transpose(bank[7][0:L+1,j*P:j*P+P],k5_e[:,j],ident[:])
                    signal(l,'k5_turned')
                if s=="linear_turn": turn(x4,b,'x4_done',bank[3],'x4T_ready')
                if s=="context_out":
                    wait_batch(pe,'k5T_done',b,1)
                    wait_batch(pe,'v5_done',b,1)
                    for j in range(4): l=mm(bank[5][:,j*P:j*P+P],k5T[:,j*P:j*P+P],v5_s[:,j*P:j*P+P])
                    signal(l,'context_ready')
                if s=="q":
                    wait_batch(pe,'x4T_done',b,1)
                    wait_batch(pe,'q5_normed',b,k)
                    signal(mm(bank[3][:],x4T[:,k*P:k*P+P],weights['Wq5'][:]),'q5_ready')
                if s=="a":
                    wait_batch(pe,'q5_exp_done',b,k+1)
                    wait_batch(pe,'q5T_done',b,k)
                    for j in range(4): l=pe.transpose(bank[7][:,j*P:j*P+P],q5_e[:,k%2,j*P:j*P+P],ident[:])
                    signal(l,'q5_turned')
                if s=="o":
                    wait_batch(pe,'q5T_done',b,k+1)
                    wait_batch(pe,'o5_done',b,k)
                    if k==0: wait_batch(pe,'context_done',b,2)
                    for j in range(4): l=mm(bank[5][:,j*P:j*P+P],q5_eT[:,j*P:j*P+P],context_s[:,j])
                    signal(l,'o5_ready')
                if s=="z":
                    wait_batch(pe,'o5_normed',b,k+1)
                    wait_batch(pe,'o5T_done',b,k)
                    for j in range(4): l=pe.transpose(bank[6][:,j*P:j*P+P],o5_n[:,k%2,j*P:j*P+P],ident[:])
                    signal(l,'o5_turned')
                if s=="w":
                    wait_batch(pe,'o5T_done',b,k+1)
                    for j in range(4): l=mm(bank[4][:,k*P:k*P+P],o5_nT[:,j*P:j*P+P],wo_gained[:,j],j==0,j==3)
                    signal(l,'second_ready')
                if s=="second_turn": turn(x5,b,'x5_done',bank[7],'x5T_ready')
                if s=="ffn_in":
                    wait_batch(pe,'xk_done',b,1)
                    signal(mm(bank[3][:],weights['Wk6'][:],xk),'k6_ready')
                    wait_batch(pe,'xr_done',b,1)
                    for t in range(4): l=mm(bank[5][:,t*P:t*P+P],xr[:,t*P:t*P+P],weights['Wr'][:])
                    signal(l,'r6_ready')
                if s=="ffn_out":
                    wait_batch(pe,'k6_squared',b,1)
                    for t in range(4): l=mm(bank[6][:,t*P:t*P+P],k6_sq[:,t*P:t*P+P],weights['Wv6'][:])
                    signal(l,'v6_ready')
            for s,b,k in ORDER: stage(s,b,k)

def host(I):
    T=lambda a: np.ascontiguousarray(a.T)
    D={}
    x=I['x'].reshape(NT*P,P)
    D['x']=x
    D['xT']=T(x)
    D['wqkv']=np.ascontiguousarray(I['L0_attn_W_qkv'].reshape(P,C,3,DH).transpose(0,2,1,3).reshape(P,3*P))
    D['bqkv']=np.ascontiguousarray(I['L0_attn_b_qkv'].reshape(C,3,DH).transpose(1,0,2).reshape(1,3*P))
    D['wout']=I['L0_attn_W_out']
    D['bout']=I['L0_attn_b_out'].reshape(1,P)
    D['ctxT']=np.ascontiguousarray(I['ctx_1024'].transpose(0,2,1))
    D['wq']=T(I['L0_xattn_wq'])
    D['wk']=T(I['L0_xattn_wk'])
    D['wv']=T(I['L0_xattn_wv'])
    D['wo']=T(I['L0_xattn_wo'])
    D['gate']=T(I['L0_ffn_gate_w'])
    D['w1']=np.ascontiguousarray(I['L0_ffn_w1'].transpose(1,0,2).reshape(P,NE*F))
    D['w2']=np.ascontiguousarray(I['L0_ffn_w2'].reshape(NE*2,P,P).transpose(1,0,2).reshape(P,NE*2*P))
    D['wkv1']=np.ascontiguousarray(np.concatenate([I['L1_attn_Wk'].T,I['L1_attn_Wv'].T],1))
    D['wq1']=T(I['L1_attn_Wq'])
    D['Wq5']=I['L1_xattn_Wq']
    D['Wk5']=np.ascontiguousarray(I['L1_xattn_Wkv'][:,:512])
    D['Wv5']=np.ascontiguousarray(I['L1_xattn_Wkv'][:,512:])
    D['Wo5']=np.ascontiguousarray(I['L1_xattn_Wout'].reshape(4,P,P).transpose(1,0,2).reshape(P,512))
    D['Wr']=T(I['L1_ffn_W_r'])
    D['Wk6']=T(I['L1_ffn_W_k'])
    D['Wv6']=T(I['L1_ffn_W_v'])
    cols=[('bq',I['L0_xattn_bq'][:,None]),('bk',I['L0_xattn_bk'][:,None]),('bq1',I['L1_attn_bq'][:,None]),('b1',I['L0_ffn_b1'].reshape(NE*2,P).T),
      ('lng',I['L1_xattn_ln_out_g'].reshape(4,P).T),('lnb',I['L1_xattn_ln_out_b'].reshape(4,P).T),('mu',np.stack([I['L1_ffn_mu_r'],I['L1_ffn_mu_k']],1)),('nk',np.tile(I['L1_xattn_null_kv'][0],2)[:,None])]
    CN={}
    o=0
    for n,a in cols: CN[n]=o;o+=a.shape[1]
    D['cols']=np.ascontiguousarray(np.concatenate([a for _,a in cols],1))
    names='wq wk wv wo gate w1 w2 wkv1 wq1 Wq5 Wk5 Wv5 Wo5 Wr Wk6 Wv6 cols'.split()
    w=np.concatenate([D.pop(n) for n in names],1)
    D['w_all']=np.ascontiguousarray(np.pad(w,((0,0),(0,-w.shape[1]%(NT-1)))))
    rows=[('bv',I['L0_xattn_bv']),('bo',I['L0_xattn_bo']),('bkv1',np.concatenate([I['L1_attn_bk'],I['L1_attn_bv']])),('gamma',I['L1_attn_gamma']),('beta',I['L1_attn_beta']),('ln_q_g',I['L1_xattn_ln_q_g']),('ln_q_b',I['L1_xattn_ln_q_b'])]
    RN={}
    o=0
    for n,a in rows: RN[n]=o;o+=a.shape[0]
    D['rows']=np.ascontiguousarray(np.concatenate([a for _,a in rows])[None])
    D['b2']=I['L0_ffn_b2']
    nk,nv=I['L1_xattn_null_kv']
    D['nv']=np.ascontiguousarray(np.tile(nv,8)[None])
    return D,CN,RN

def kernel(**inputs):
    import concourse.bacc as bacc
    from concourse.bass_utils import run_bass_kernel_spmd
    D,CN,RN=host({k:np.asarray(v) for k,v in inputs.items()})
    nc=bacc.Bacc("TRN2", target_bir_lowering=False, num_devices=1)
    arrays={"in_"+k:np.ascontiguousarray(v) for k,v in D.items()}
    aps={k:nc.dram_tensor("in_"+k, arrays["in_"+k].shape, mybir.dt.from_np(arrays["in_"+k].dtype), kind="ExternalInput").ap() for k in D}
    out=nc.dram_tensor("out_x", (NB,NQ,P), F32, kind="ExternalOutput").ap()
    build(nc, CN, RN, out, aps)
    r=run_bass_kernel_spmd(nc, [arrays], core_ids=[0])
    return r.results[0]["out_x"]
```
